# Optimizing a Trainium2 kernel written in Bass

```python
import numpy as np
import jax
import jax.numpy as jnp

def _softmax(x, axis=-1):
    return jax.nn.softmax(x, axis=axis)

def _gelu(x):
    return jax.nn.gelu(x, approximate=True)

def _silu(x):
    return jax.nn.silu(x)

def _sigmoid(x):
    return jax.nn.sigmoid(x)

def _layernorm(x, axis=-1, eps=1e-05):
    m = jnp.mean(x, axis=axis, keepdims=True)
    v = jnp.var(x, axis=axis, keepdims=True)
    return (x - m) / jnp.sqrt(v + eps)

def _scatter_add(tgt, idx, src, axis=0):
    return tgt.at[idx].add(src)

def _segment_sum(src, seg, n):
    return jax.ops.segment_sum(src, seg, n)
kernel_name = 'mk_cond_seq_d4_seqx_r4_2796f5'

def setup_inputs(seed: int=0):
    np.random.seed(seed)
    _w = jnp.asarray

    def _rec_inputs():
        import jax
        import jax.numpy as jnp
        _rk = jax.random.key(seed)
        x = 1.648e-05 + 1 * jax.random.normal(jax.random.fold_in(_rk, 1), (4, 512, 288), jnp.float32)
        _lenS = 512 - jax.random.randint(jax.random.fold_in(_rk, 7), (4,), 0, max(1, 512 // 4) + 1, jnp.int32)
        _lenS2 = 512 - jax.random.randint(jax.random.fold_in(_rk, 8), (4,), 0, max(1, 512 // 4) + 1, jnp.int32)
        cond_1152 = 0.00914911 + 1.00357 * jax.random.normal(jax.random.fold_in(_rk, 11), (4, 288), jnp.float32)
        return (x, cond_1152)
    x, cond_1152 = _rec_inputs()

    def _L0_cond_setup():
        import jax, jax.numpy as jnp
        import numpy as np
        NUM_HEADS = 16
        NUM_EXPERTS = 4
        TOP_K = 2
        LN_EPS = 1e-06

        def _ln(h):
            mu = jnp.mean(h, axis=-1, keepdims=True)
            var = jnp.var(h, axis=-1, keepdims=True)
            return (h - mu) * jax.lax.rsqrt(var + LN_EPS)

        def _modulate(h, shift, scale):
            return h * (1.0 + scale[:, None, :]) + shift[:, None, :]
        key = jax.random.key(seed)
        ks = jax.random.split(key, 12)
        B, N, C = (8, 256, 288)
        H = 4 * C
        E = NUM_EXPERTS
        s = 0.02
        return {'x': jax.random.normal(ks[0], (B, N, C), jnp.float32), 'c': jax.random.normal(ks[1], (B, C), jnp.float32), 'w_adaln': jax.random.normal(ks[2], (C, 6 * C), jnp.float32) * s, 'b_adaln': jnp.zeros((6 * C,), jnp.float32), 'w_qkv': jax.random.normal(ks[3], (C, 3 * C), jnp.float32) * s, 'b_qkv': jnp.zeros((3 * C,), jnp.float32), 'w_proj': jax.random.normal(ks[4], (C, C), jnp.float32) * s, 'b_proj': jnp.zeros((C,), jnp.float32), 'w_gate': jax.random.normal(ks[5], (C, E), jnp.float32) * s, 'w1': jax.random.normal(ks[6], (E, C, H), jnp.float32) * s, 'b1': jnp.zeros((E, H), jnp.float32), 'w2': jax.random.normal(ks[7], (E, H, C), jnp.float32) * s, 'b2': jnp.zeros((E, C), jnp.float32)}
    _L0_cond_all = _L0_cond_setup()
    _L0_cond_in = {k: v for k, v in _L0_cond_all.items() if k in ('w_adaln', 'b_adaln', 'w_qkv', 'b_qkv', 'w_proj', 'b_proj', 'w_gate', 'w1', 'b1', 'w2', 'b2')}
    del _L0_cond_all

    def _L1_cond_setup():
        import jax, jax.numpy as jnp
        import numpy as np
        B, L, C = (8, 256, 288)
        H = 16
        D = C // H
        FF = int(C * 4.0)
        EPS = 1e-06

        def _layernorm(x):
            mu = jnp.mean(x, axis=-1, keepdims=True)
            var = jnp.mean(jnp.square(x - mu), axis=-1, keepdims=True)
            return (x - mu) * jax.lax.rsqrt(var + EPS)

        def _modulate(x, shift, scale):
            return x * (1.0 + scale) + shift

        def _attention(h, W_qkv, b_qkv, W_proj, b_proj):
            b, l, c = h.shape
            qkv = h @ W_qkv + b_qkv
            qkv = qkv.reshape(b, l, 3, H, D)
            q, k, v = (qkv[:, :, 0], qkv[:, :, 1], qkv[:, :, 2])
            scale = D ** (-0.5)
            scores = jnp.einsum('blhd,bmhd->bhlm', q * scale, k)
            attn = jax.nn.softmax(scores, axis=-1)
            o = jnp.einsum('bhlm,bmhd->blhd', attn, v).reshape(b, l, c)
            return o @ W_proj + b_proj
        key = jax.random.key(seed)
        ks = jax.random.split(key, 12)
        s = 0.02
        return {'x': jax.random.normal(ks[0], (B, L, C), jnp.float32), 'c': jax.random.normal(ks[1], (B, 1, C), jnp.float32), 'W_qkv': jax.random.normal(ks[2], (C, 3 * C), jnp.float32) * s, 'b_qkv': jnp.zeros((3 * C,), jnp.float32), 'W_proj': jax.random.normal(ks[3], (C, C), jnp.float32) * s, 'b_proj': jnp.zeros((C,), jnp.float32), 'W_fc1': jax.random.normal(ks[4], (C, FF), jnp.float32) * s, 'b_fc1': jnp.zeros((FF,), jnp.float32), 'W_fc2': jax.random.normal(ks[5], (FF, C), jnp.float32) * s, 'b_fc2': jnp.zeros((C,), jnp.float32), 'W_ada': jax.random.normal(ks[6], (C, 6 * C), jnp.float32) * s, 'b_ada': jnp.zeros((6 * C,), jnp.float32)}
    _L1_cond_all = _L1_cond_setup()
    _L1_cond_in = {k: v for k, v in _L1_cond_all.items() if k in ('W_qkv', 'b_qkv', 'W_proj', 'b_proj', 'W_fc1', 'b_fc1', 'W_fc2', 'b_fc2', 'W_ada', 'b_ada')}
    del _L1_cond_all

    def _L2_cond_setup():
        import jax, jax.numpy as jnp
        import numpy as np
        N, T, D, H = (32, 256, 288, 16)
        DH = D // H
        MLP = int(D * 4.0)
        EPS = 1e-06

        def _layernorm(x):
            m = jnp.mean(x, axis=-1, keepdims=True)
            v = jnp.var(x, axis=-1, keepdims=True)
            return (x - m) * jax.lax.rsqrt(v + EPS)

        def _modulate(x, shift, scale):
            return x * (1.0 + scale[:, None, :]) + shift[:, None, :]

        def _attention(x, qkv_w, qkv_b, proj_w, proj_b):
            n, t, d = x.shape
            scale = DH ** (-0.5)
            qkv = x @ qkv_w + qkv_b
            qkv = qkv.reshape(n, t, 3, H, DH)
            q, k, v = (qkv[:, :, 0], qkv[:, :, 1], qkv[:, :, 2])
            attn = jnp.einsum('nthd,ntkd->nthk', q * scale, k)
            attn = jax.nn.softmax(attn, axis=-1)
            out = jnp.einsum('nthk,ntkd->nthd', attn, v)
            out = out.transpose(0, 2, 1, 3).reshape(n, t, d)
            return out @ proj_w + proj_b

        def _mlp(x, fc1_w, fc1_b, fc2_w, fc2_b):
            h = jax.nn.gelu(x @ fc1_w + fc1_b, approximate=False)
            return h @ fc2_w + fc2_b
        key = jax.random.key(seed)
        ks = jax.random.split(key, 14)
        s = 0.02
        return {'x': jax.random.normal(ks[0], (N, T, D), jnp.float32), 'c': jax.random.normal(ks[1], (N, D), jnp.float32), 'qkv_w': jax.random.normal(ks[2], (D, 3 * D), jnp.float32) * s, 'qkv_b': jax.random.normal(ks[3], (3 * D,), jnp.float32) * s, 'proj_w': jax.random.normal(ks[4], (D, D), jnp.float32) * s, 'proj_b': jax.random.normal(ks[5], (D,), jnp.float32) * s, 'fc1_w': jax.random.normal(ks[6], (D, MLP), jnp.float32) * s, 'fc1_b': jax.random.normal(ks[7], (MLP,), jnp.float32) * s, 'fc2_w': jax.random.normal(ks[8], (MLP, D), jnp.float32) * s, 'fc2_b': jax.random.normal(ks[9], (D,), jnp.float32) * s, 'ada_w': jax.random.normal(ks[10], (D, 6 * D), jnp.float32) * s, 'ada_b': jax.random.normal(ks[11], (6 * D,), jnp.float32) * s}
    _L2_cond_all = _L2_cond_setup()
    _L2_cond_in = {k: v for k, v in _L2_cond_all.items() if k in ('qkv_w', 'qkv_b', 'proj_w', 'proj_b', 'fc1_w', 'fc1_b', 'fc2_w', 'fc2_b', 'ada_w', 'ada_b')}
    del _L2_cond_all

    def _L3_cond_setup():
        import math
        import jax, jax.numpy as jnp
        import numpy as np
        B, T, D = (8, 256, 288)
        H = 16
        E = 4
        EPS = 1e-06

        def _layer_norm(x):
            mu = jnp.mean(x, axis=-1, keepdims=True)
            var = jnp.mean(jnp.square(x - mu), axis=-1, keepdims=True)
            return (x - mu) * jax.lax.rsqrt(var + EPS)

        def _modulate(x, shift, scale):
            return x * (1.0 + scale) + shift

        def _attention(y, qkv_w, qkv_b, out_w, out_b):
            b, t, d = y.shape
            hd = d // H
            qkv = y @ qkv_w + qkv_b
            q, k, v = jnp.split(qkv, 3, axis=-1)
            q = q.reshape(b, t, H, hd).transpose(0, 2, 1, 3)
            k = k.reshape(b, t, H, hd).transpose(0, 2, 1, 3)
            v = v.reshape(b, t, H, hd).transpose(0, 2, 1, 3)
            scores = jnp.einsum('bhqd,bhkd->bhqk', q, k) / math.sqrt(hd)
            attn = jax.nn.softmax(scores, axis=-1)
            out = jnp.einsum('bhqk,bhkd->bhqd', attn, v)
            out = out.transpose(0, 2, 1, 3).reshape(b, t, d)
            return out @ out_w + out_b
        key = jax.random.key(seed)
        ks = jax.random.split(key, 12)
        std = 0.02
        return {'x': jax.random.normal(ks[0], (B, T, D), dtype=jnp.float32), 'c': jax.random.normal(ks[1], (B, D), dtype=jnp.float32), 'qkv_w': jax.random.normal(ks[2], (D, 3 * D), dtype=jnp.float32) * std, 'qkv_b': jnp.zeros((3 * D,), dtype=jnp.float32), 'out_w': jax.random.normal(ks[3], (D, D), dtype=jnp.float32) * std, 'out_b': jnp.zeros((D,), dtype=jnp.float32), 'w1': jax.random.normal(ks[4], (D, E * D), dtype=jnp.float32) * std, 'b1': jnp.zeros((E * D,), dtype=jnp.float32), 'w2': jax.random.normal(ks[5], (E * D, D), dtype=jnp.float32) * std, 'b2': jnp.zeros((D,), dtype=jnp.float32), 'ada_w': jax.random.normal(ks[6], (D, 6 * D), dtype=jnp.float32) * std, 'ada_b': jnp.zeros((6 * D,), dtype=jnp.float32)}
    _L3_cond_all = _L3_cond_setup()
    _L3_cond_in = {k: v for k, v in _L3_cond_all.items() if k in ('qkv_w', 'qkv_b', 'out_w', 'out_b', 'w1', 'b1', 'w2', 'b2', 'ada_w', 'ada_b')}
    del _L3_cond_all
    return {'x': x, 'cond_1152': cond_1152, 'L0_cond_w_adaln': _L0_cond_in['w_adaln'], 'L0_cond_b_adaln': _L0_cond_in['b_adaln'], 'L0_cond_w_qkv': _L0_cond_in['w_qkv'], 'L0_cond_b_qkv': _L0_cond_in['b_qkv'], 'L0_cond_w_proj': _L0_cond_in['w_proj'], 'L0_cond_b_proj': _L0_cond_in['b_proj'], 'L0_cond_w_gate': _L0_cond_in['w_gate'], 'L0_cond_w1': _L0_cond_in['w1'], 'L0_cond_b1': _L0_cond_in['b1'], 'L0_cond_w2': _L0_cond_in['w2'], 'L0_cond_b2': _L0_cond_in['b2'], 'L1_cond_W_qkv': _L1_cond_in['W_qkv'], 'L1_cond_b_qkv': _L1_cond_in['b_qkv'], 'L1_cond_W_proj': _L1_cond_in['W_proj'], 'L1_cond_b_proj': _L1_cond_in['b_proj'], 'L1_cond_W_fc1': _L1_cond_in['W_fc1'], 'L1_cond_b_fc1': _L1_cond_in['b_fc1'], 'L1_cond_W_fc2': _L1_cond_in['W_fc2'], 'L1_cond_b_fc2': _L1_cond_in['b_fc2'], 'L1_cond_W_ada': _L1_cond_in['W_ada'], 'L1_cond_b_ada': _L1_cond_in['b_ada'], 'L2_cond_qkv_w': _L2_cond_in['qkv_w'], 'L2_cond_qkv_b': _L2_cond_in['qkv_b'], 'L2_cond_proj_w': _L2_cond_in['proj_w'], 'L2_cond_proj_b': _L2_cond_in['proj_b'], 'L2_cond_fc1_w': _L2_cond_in['fc1_w'], 'L2_cond_fc1_b': _L2_cond_in['fc1_b'], 'L2_cond_fc2_w': _L2_cond_in['fc2_w'], 'L2_cond_fc2_b': _L2_cond_in['fc2_b'], 'L2_cond_ada_w': _L2_cond_in['ada_w'], 'L2_cond_ada_b': _L2_cond_in['ada_b'], 'L3_cond_qkv_w': _L3_cond_in['qkv_w'], 'L3_cond_qkv_b': _L3_cond_in['qkv_b'], 'L3_cond_out_w': _L3_cond_in['out_w'], 'L3_cond_out_b': _L3_cond_in['out_b'], 'L3_cond_w1': _L3_cond_in['w1'], 'L3_cond_b1': _L3_cond_in['b1'], 'L3_cond_w2': _L3_cond_in['w2'], 'L3_cond_b2': _L3_cond_in['b2'], 'L3_cond_ada_w': _L3_cond_in['ada_w'], 'L3_cond_ada_b': _L3_cond_in['ada_b']}

def reference(x, cond_1152, L0_cond_w_adaln, L0_cond_b_adaln, L0_cond_w_qkv, L0_cond_b_qkv, L0_cond_w_proj, L0_cond_b_proj, L0_cond_w_gate, L0_cond_w1, L0_cond_b1, L0_cond_w2, L0_cond_b2, L1_cond_W_qkv, L1_cond_b_qkv, L1_cond_W_proj, L1_cond_b_proj, L1_cond_W_fc1, L1_cond_b_fc1, L1_cond_W_fc2, L1_cond_b_fc2, L1_cond_W_ada, L1_cond_b_ada, L2_cond_qkv_w, L2_cond_qkv_b, L2_cond_proj_w, L2_cond_proj_b, L2_cond_fc1_w, L2_cond_fc1_b, L2_cond_fc2_w, L2_cond_fc2_b, L2_cond_ada_w, L2_cond_ada_b, L3_cond_qkv_w, L3_cond_qkv_b, L3_cond_out_w, L3_cond_out_b, L3_cond_w1, L3_cond_b1, L3_cond_w2, L3_cond_b2, L3_cond_ada_w, L3_cond_ada_b):
    import jax
    import jax.numpy as jnp

    def _L0_cond_ref(x, c, w_adaln, b_adaln, w_qkv, b_qkv, w_proj, b_proj, w_gate, w1, b1, w2, b2):
        import jax, jax.numpy as jnp
        import numpy as np
        NUM_HEADS = 16
        NUM_EXPERTS = 4
        TOP_K = 2
        LN_EPS = 1e-06

        def _ln(h):
            mu = jnp.mean(h, axis=-1, keepdims=True)
            var = jnp.var(h, axis=-1, keepdims=True)
            return (h - mu) * jax.lax.rsqrt(var + LN_EPS)

        def _modulate(h, shift, scale):
            return h * (1.0 + scale[:, None, :]) + shift[:, None, :]
        B, N, C = x.shape
        nh = NUM_HEADS
        hd = C // nh
        mod = jax.nn.silu(c) @ w_adaln + b_adaln
        sh_msa, sc_msa, g_msa, sh_mlp, sc_mlp, g_mlp = jnp.split(mod, 6, axis=-1)
        h = _modulate(_ln(x), sh_msa, sc_msa)
        qkv = (h @ w_qkv + b_qkv).reshape(B, N, 3, nh, hd).transpose(2, 0, 3, 1, 4)
        q, k, v = (qkv[0], qkv[1], qkv[2])
        attn = jax.nn.softmax(jnp.einsum('bhqd,bhkd->bhqk', q, k) * hd ** (-0.5), axis=-1)
        o = jnp.einsum('bhqk,bhkd->bhqd', attn, v).transpose(0, 2, 1, 3).reshape(B, N, C)
        o = o @ w_proj + b_proj
        x = x + g_msa[:, None, :] * o
        xn = _modulate(_ln(x), sh_mlp, sc_mlp)
        xf = xn.reshape(-1, C)
        gate_logits = xf @ w_gate
        topk_logits, topk_idx = jax.lax.top_k(gate_logits, TOP_K)
        gates = jax.nn.softmax(topk_logits, axis=-1)
        cw = jnp.sum(jax.nn.one_hot(topk_idx, NUM_EXPERTS, dtype=xf.dtype) * gates[..., None], axis=1)
        hmid = jax.nn.gelu(jnp.einsum('tc,ech->eth', xf, w1) + b1[:, None, :], approximate=True)
        eo = jnp.einsum('eth,ehc->etc', hmid, w2) + b2[:, None, :]
        moe = jnp.einsum('te,etc->tc', cw, eo).reshape(B, N, C)
        return x + g_mlp[:, None, :] * moe

    def _L1_cond_ref(x, c, W_qkv, b_qkv, W_proj, b_proj, W_fc1, b_fc1, W_fc2, b_fc2, W_ada, b_ada):
        import jax, jax.numpy as jnp
        import numpy as np
        B, L, C = (8, 256, 288)
        H = 16
        D = C // H
        FF = int(C * 4.0)
        EPS = 1e-06

        def _layernorm(x):
            mu = jnp.mean(x, axis=-1, keepdims=True)
            var = jnp.mean(jnp.square(x - mu), axis=-1, keepdims=True)
            return (x - mu) * jax.lax.rsqrt(var + EPS)

        def _modulate(x, shift, scale):
            return x * (1.0 + scale) + shift

        def _attention(h, W_qkv, b_qkv, W_proj, b_proj):
            b, l, c = h.shape
            qkv = h @ W_qkv + b_qkv
            qkv = qkv.reshape(b, l, 3, H, D)
            q, k, v = (qkv[:, :, 0], qkv[:, :, 1], qkv[:, :, 2])
            scale = D ** (-0.5)
            scores = jnp.einsum('blhd,bmhd->bhlm', q * scale, k)
            attn = jax.nn.softmax(scores, axis=-1)
            o = jnp.einsum('bhlm,bmhd->blhd', attn, v).reshape(b, l, c)
            return o @ W_proj + b_proj
        ada = jax.nn.silu(c) @ W_ada + b_ada
        shift_msa, scale_msa, gate_msa, shift_mlp, scale_mlp, gate_mlp = jnp.split(ada, 6, axis=-1)
        h = _modulate(_layernorm(x), shift_msa, scale_msa)
        x = x + gate_msa * _attention(h, W_qkv, b_qkv, W_proj, b_proj)
        h = _modulate(_layernorm(x), shift_mlp, scale_mlp)
        mlp = jax.nn.gelu(h @ W_fc1 + b_fc1, approximate=True) @ W_fc2 + b_fc2
        x = x + gate_mlp * mlp
        return x

    def _L2_cond_ref(x, c, qkv_w, qkv_b, proj_w, proj_b, fc1_w, fc1_b, fc2_w, fc2_b, ada_w, ada_b):
        import jax, jax.numpy as jnp
        import numpy as np
        N, T, D, H = (32, 256, 288, 16)
        DH = D // H
        MLP = int(D * 4.0)
        EPS = 1e-06

        def _layernorm(x):
            m = jnp.mean(x, axis=-1, keepdims=True)
            v = jnp.var(x, axis=-1, keepdims=True)
            return (x - m) * jax.lax.rsqrt(v + EPS)

        def _modulate(x, shift, scale):
            return x * (1.0 + scale[:, None, :]) + shift[:, None, :]

        def _attention(x, qkv_w, qkv_b, proj_w, proj_b):
            n, t, d = x.shape
            scale = DH ** (-0.5)
            qkv = x @ qkv_w + qkv_b
            qkv = qkv.reshape(n, t, 3, H, DH)
            q, k, v = (qkv[:, :, 0], qkv[:, :, 1], qkv[:, :, 2])
            attn = jnp.einsum('nthd,ntkd->nthk', q * scale, k)
            attn = jax.nn.softmax(attn, axis=-1)
            out = jnp.einsum('nthk,ntkd->nthd', attn, v)
            out = out.transpose(0, 2, 1, 3).reshape(n, t, d)
            return out @ proj_w + proj_b

        def _mlp(x, fc1_w, fc1_b, fc2_w, fc2_b):
            h = jax.nn.gelu(x @ fc1_w + fc1_b, approximate=False)
            return h @ fc2_w + fc2_b
        ada = jax.nn.silu(c) @ ada_w + ada_b
        shift_msa, scale_msa, gate_msa, shift_mlp, scale_mlp, gate_mlp = jnp.split(ada, 6, axis=1)
        x = x + gate_msa[:, None, :] * _attention(_modulate(_layernorm(x), shift_msa, scale_msa), qkv_w, qkv_b, proj_w, proj_b)
        x = x + gate_mlp[:, None, :] * _mlp(_modulate(_layernorm(x), shift_mlp, scale_mlp), fc1_w, fc1_b, fc2_w, fc2_b)
        return x

    def _L3_cond_ref(x, c, qkv_w, qkv_b, out_w, out_b, w1, b1, w2, b2, ada_w, ada_b):
        import math
        import jax, jax.numpy as jnp
        import numpy as np
        B, T, D = (8, 256, 288)
        H = 16
        E = 4
        EPS = 1e-06

        def _layer_norm(x):
            mu = jnp.mean(x, axis=-1, keepdims=True)
            var = jnp.mean(jnp.square(x - mu), axis=-1, keepdims=True)
            return (x - mu) * jax.lax.rsqrt(var + EPS)

        def _modulate(x, shift, scale):
            return x * (1.0 + scale) + shift

        def _attention(y, qkv_w, qkv_b, out_w, out_b):
            b, t, d = y.shape
            hd = d // H
            qkv = y @ qkv_w + qkv_b
            q, k, v = jnp.split(qkv, 3, axis=-1)
            q = q.reshape(b, t, H, hd).transpose(0, 2, 1, 3)
            k = k.reshape(b, t, H, hd).transpose(0, 2, 1, 3)
            v = v.reshape(b, t, H, hd).transpose(0, 2, 1, 3)
            scores = jnp.einsum('bhqd,bhkd->bhqk', q, k) / math.sqrt(hd)
            attn = jax.nn.softmax(scores, axis=-1)
            out = jnp.einsum('bhqk,bhkd->bhqd', attn, v)
            out = out.transpose(0, 2, 1, 3).reshape(b, t, d)
            return out @ out_w + out_b
        mods = (jax.nn.silu(c) @ ada_w + ada_b)[:, None, :]
        m0, m1, m2, m3, m4, m5 = jnp.split(mods, 6, axis=-1)
        y = _modulate(_layer_norm(x), m0, m1)
        x = x + m2 * _attention(y, qkv_w, qkv_b, out_w, out_b)
        y = _modulate(_layer_norm(x), m3, m4)
        y = jax.nn.gelu(y @ w1 + b1, approximate=True)
        x = x + m5 * (y @ w2 + b2)
        return x
    x = _L0_cond_ref(x, cond_1152, L0_cond_w_adaln, L0_cond_b_adaln, L0_cond_w_qkv, L0_cond_b_qkv, L0_cond_w_proj, L0_cond_b_proj, L0_cond_w_gate, L0_cond_w1, L0_cond_b1, L0_cond_w2, L0_cond_b2)
    x = _L1_cond_ref(x, cond_1152[:, None, :], L1_cond_W_qkv, L1_cond_b_qkv, L1_cond_W_proj, L1_cond_b_proj, L1_cond_W_fc1, L1_cond_b_fc1, L1_cond_W_fc2, L1_cond_b_fc2, L1_cond_W_ada, L1_cond_b_ada)
    x = _L2_cond_ref(x, cond_1152, L2_cond_qkv_w, L2_cond_qkv_b, L2_cond_proj_w, L2_cond_proj_b, L2_cond_fc1_w, L2_cond_fc1_b, L2_cond_fc2_w, L2_cond_fc2_b, L2_cond_ada_w, L2_cond_ada_b)
    x = _L3_cond_ref(x, cond_1152, L3_cond_qkv_w, L3_cond_qkv_b, L3_cond_out_w, L3_cond_out_b, L3_cond_w1, L3_cond_b1, L3_cond_w2, L3_cond_b2, L3_cond_ada_w, L3_cond_ada_b)
    return x

_drawn_inputs = setup_inputs


def setup_inputs(seed=0):
    import zlib

    import numpy as np

    out = dict(_drawn_inputs(seed))
    spreads = {'L0_cond_b_adaln': (0.0, 0.431),
     'L0_cond_b_qkv': (0.0, 0.8),
     'L0_cond_b_proj': (0.0, 0.355),
     'L0_cond_b1': (0.0, 0.8),
     'L0_cond_b2': (0.0, 0.511),
     'L1_cond_b_qkv': (0.0, 0.8),
     'L1_cond_b_proj': (0.0, 0.337),
     'L1_cond_b_fc1': (0.0, 0.8),
     'L1_cond_b_fc2': (0.0, 0.358),
     'L1_cond_b_ada': (0.0, 0.376),
     'L3_cond_qkv_b': (0.0, 0.8),
     'L3_cond_out_b': (0.0, 0.402),
     'L3_cond_b1': (0.0, 0.8),
     'L3_cond_b2': (0.0, 0.348),
     'L3_cond_ada_b': (0.0, 0.384)}
    factors = {'L0_cond_w_qkv': 8.0,
     'L0_cond_w_proj': 5.501,
     'L0_cond_w_gate': 2.866,
     'L0_cond_w1': 2.709,
     'L1_cond_W_qkv': 8.0,
     'L1_cond_W_proj': 5.44,
     'L2_cond_qkv_w': 8.0,
     'L2_cond_qkv_b': 8.0,
     'L2_cond_proj_w': 8.0,
     'L2_cond_proj_b': 31.804,
     'L2_cond_fc1_b': 64.0,
     'L2_cond_fc2_b': 31.431,
     'L2_cond_ada_b': 8.0,
     'L3_cond_qkv_w': 8.0,
     'L3_cond_out_w': 5.938,
     'L2_cond_fc1_w': 4.248,
     'L2_cond_fc2_w': 4.035,
     'L3_cond_w1': 3.609}
    for name, (base, spread) in spreads.items():
        noise = np.random.default_rng([zlib.crc32(name.encode()), seed]).standard_normal(out[name].shape)
        drawn = base * np.exp(spread * noise) if base else spread * noise
        out[name] = jnp.asarray(drawn.astype(out[name].dtype))
    for name, factor in factors.items():
        out[name] = (out[name] * factor).astype(out[name].dtype)
    return out
```

```python
import numpy as np
import concourse.bass as bass
from concourse import mybir
from contextlib import ExitStack

F32 = mybir.dt.float32
F32R = mybir.dt.float32r
ALU = mybir.AluOpType
ACT = mybir.ActivationFunctionType
AX = mybir.AxisListType

B, T, C, H, D = 4, 512, 288, 16, 18
QT = T // 128
NI = 16
NE = 4
NCH = 9
V1 = D + 1
SCALE = float(D) ** -0.5
EPS = 1e-6
R2 = 98
CW_ = 256 + 3 * 32


def r(ap):
    return ap.bitcast(F32R)


def view(ap, part, free, dims):
    step = ap.ap[0][0]
    return bass.AP(ap.tensor, ap.offset + part * step + free,
                   [[s * step if isp else s, n] for s, n, isp in dims])


class Count:

    def __init__(self, sem, step=1):
        self.sem, self.step, self.n = sem, step, 0


class Queue:

    def __init__(self, done=None):
        self.items, self.seen, self.done = [], {}, done

    def wait(self, *marks):
        for m in marks:
            if m is None:
                continue
            if isinstance(m, list):
                self.wait(*m)
                continue
            c, v = m
            if self.seen.get(id(c), 0) < v:
                self.seen[id(c)] = v
                self.items.append(lambda e, c=c, v=v: e.wait_ge(c.sem, v))

    def do(self, fn, *marks, sig=None, end=True):
        self.wait(*marks)
        if not end:
            self.items.append(fn)
            return None
        c = sig or self.done
        c.n += c.step
        self.items.append(lambda e: fn(e).then_inc(c.sem, c.step))
        return (c, c.n)

    def run(self, e):
        for f in self.items:
            f(e)


def build(nc, x_in, cond, layers, gate_w, out):
    ctx = ExitStack()
    with ctx:
        def sb(name, shape):
            return ctx.enter_context(nc.sbuf_tensor(name, shape, F32))

        def sem(name, step=1):
            return Count(ctx.enter_context(nc.semaphore(name)), step)

        X = sb("X", [128, B * QT, C])
        A = [sb(f"A{n}", [128, 5, T]) for n in range(2)]
        WQ = sb("WQ", [128, 3, 2 * C])
        WQL = sb("WQL", [128, 2, 2 * C])
        WV = sb("WV", [128, 3, C])
        WVL = sb("WVL", [128, 2, C])
        WP = sb("WP", [128, 3, C])
        WPL = sb("WPL", [128, 2, C])
        NSC = 3 * (3 * 128) + 3 * C
        NLC = 2 * (3 * 128) + 3 * C
        FH = [sb(f"FH{n}", [128, NSC]) for n in range(3)]
        FL = [sb(f"FL{n}", [128, NLC]) for n in range(3)]
        ST = [sb(f"ST{n}", [128, NSC]) for n in range(2)]
        B2 = [sb(f"B2{n}", [2, C]) for n in range(2)]
        B2S = sb("B2S", [2, C])
        HF = [sb(f"HF{n}", [128, T]) for n in range(2)]
        HH = [sb(f"HH{n}", [128, 2, T]) for n in range(3)]
        QS = sb("QS", [128, 8, T])
        KS = sb("KS", [128, 8, T])
        VT = sb("VT", [128, QT, H * V1 + 13])
        PB = [sb(f"PB{n}", [128, 4, T]) for n in range(3)]
        OT = sb("OT", [128, QT, CW_])
        XN = sb("XN", [128, QT, CW_])
        TM = [sb(f"TM{n}", [128, C]) for n in range(2)]
        GB = sb("GB", [128, 2, C])
        GR = sb("GR", [36, 2, C])
        MF = [sb(f"MF{n}", [128, 4, 3, 4]) for n in range(2)]
        ID = sb("ID", [128, 128])
        ON = sb("ON", [2, 128])
        CT = sb("CT", [128, 3, 4])
        SL = sb("SL", [128, 3, 4])
        BN = sb("BN", [128, QT, 6])
        MV = sb("MV", [128, QT, 2])
        RS = sb("RS", [128, QT])
        VV = sb("VV", [128, 2, QT])
        OS = sb("OS", [128, T])
        MX = [sb(f"MX{n}", [128, 16]) for n in range(2)]
        M2 = [sb("M2", [16, 2, 128])] * 2
        RD = sb("RD", [128, 16])
        WG = sb("WG", [128, 3, 4])
        WGL = sb("WGL", [128, 2, 4])
        GL = sb("GL", [128, QT, 4])
        GK = sb("GK", [128, QT, 4])
        GC = sb("GC", [128, QT, 4])
        GE = sb("GE", [128, QT, 4])
        CW = sb("CW", [128, QT, 4])
        GM = sb("GM", [128, QT])
        GS = sb("GS", [128, QT])
        PS = [ctx.enter_context(nc.psum_tensor(f"PS{n}", [128, 512], F32)) for n in range(8)]
        qkd = nc.dram_tensor("qkd", [2, 2, 2 * C, T], F32, kind="Internal").ap()
        scr = nc.dram_tensor("scr", [B, H * T * D], F32, kind="Internal").ap()

        s_pe, s_act, s_dve, s_pool = sem("s_pe"), sem("s_act"), sem("s_dve"), sem("s_pool")
        s_x = [sem(f"s_x{b}", 16) for b in range(B)]
        s_c = sem("s_c", 16)
        s_g = sem("s_g", 16)
        s_st = [sem(f"s_st{n}", 16) for n in range(2)]
        s_b2 = sem("s_b2", 16)
        s_qk = [sem(f"s_qk{n}", 16) for n in range(2)]
        s_qw = sem("s_qw", 16)
        s_m = [sem(f"s_m{n}", 16) for n in range(4)]
        s_sw = [sem(f"s_sw{n}", 16) for n in range(2)]
        s_sr = sem("s_sr", 16)
        s_out = sem("s_out", 16)

        pe, act, dve, pool, sp = Queue(s_pe), Queue(s_act), Queue(s_dve), Queue(s_pool), Queue()

        bank = [None] * 8

        m = pool.do(lambda e: e.memset(ID[:, :], 0.0))
        k_id = pool.do(lambda e: e.affine_select(out=ID[:, :], in_=ID[:, :], compare_op=ALU.not_equal,
                                                 fill=1.0, base=0, pattern=[[-1, 128]],
                                                 channel_multiplier=1), m)
        k_on = pool.do(lambda e: e.memset(ON[:, :], 1.0))
        k_st = [pool.do(lambda e, n=n: e.memset(ST[n][:, :], 0.0)) for n in range(2)]
        k_ct = pool.do(lambda e: e.memset(CT[:, :, :], 0.0))
        k_sl = pool.do(lambda e: e.memset(SL[:, :, :], 1.0))
        k_a = [pool.do(lambda e, n=n: e.memset(A[n][:, 4, :], 1.0)) for n in range(2)]
        k_ks = pool.do(lambda e: e.memset(KS[:, :, :], 1.0))
        k_vt = pool.do(lambda e: e.memset(VT[:, :, :], 1.0))

        m_c = None
        for c in range(3):
            n = 128 if c < 2 else 32
            m_c = sp.do(lambda e, c=c, n=n: e.dma_start(
                CT[0:n, c, :], cond[:, c * 128:c * 128 + n].rearrange("b k -> k b"),
                allow_slow_non_contiguous=True), k_ct, sig=s_c)
        m_sl = act.do(lambda e: e.activation(SL[:, 0:2, :], CT[:, 0:2, :], ACT.Silu), m_c, k_sl)
        m_sl = act.do(lambda e: e.activation(SL[0:32, 2, :], CT[0:32, 2, :], ACT.Silu))
        x_v = x_in.rearrange("b (q p) c -> b p q c", p=128)
        m_x = [None] * B

        def load_x(b):
            m = sp.do(lambda e, b=b: e.dma_start(X[:, b * QT:(b + 1) * QT, :], x_v[b]), sig=s_x[b])
            m_x[b] = [m] * QT

        st_n = [0]
        st_free = [k_st[0], k_st[1]]

        def stage(loads):
            n = st_n[0] % 2
            st_n[0] += 1
            for dst, src in loads:
                m = sp.do(lambda e, dst=dst, src=src, n=n: e.dma_start(dst(ST[n]), src),
                          st_free[n], sig=s_st[n])
            return n, m

        def w_loads(w, bias, c0, ncol, o0, o1, o2):
            def two(s):
                return view(s[:, :], 0, o0, [(1, 128, True), (o1 - o0, 2, False), (1, ncol, False)])
            return [
                (two, w[0:256, c0:c0 + ncol].rearrange("(a p) n -> p a n", a=2)),
                (lambda s: s[0:96, o2:o2 + ncol],
                 w[256:288, c0:c0 + ncol].unsqueeze(0).to_broadcast([3, 32, ncol])),
                (lambda s: s[96:98, o2:o2 + ncol],
                 bias[:, c0:c0 + ncol].to_broadcast([2, ncol])),
            ]

        def split(n, m_ld, hi, lo, nh, nl, fix, free):
            mh = dve.do(lambda e: e.tensor_copy(r(hi), ST[n][:, 0:nh]), m_ld, free)
            ml = pool.do(lambda e: e.tensor_tensor(r(lo), ST[n][:, 0:nl], hi[:, 0:nl], ALU.subtract), mh, free)
            f0, nf = fix
            m1 = dve.do(lambda e: e.tensor_tensor(r(hi[64:R2, f0:f0 + nf]), ST[n][64:R2, f0:f0 + nf],
                                                  hi[64:R2, f0:f0 + nf], ALU.subtract), mh, ml)
            m2 = dve.do(lambda e: e.tensor_copy(r(hi[96:97, f0:f0 + nf]), ST[n][96:97, f0:f0 + nf]), m1)
            st_free[n] = [ml, m2]
            return [ml, m2]

        m_wq, m_wv = [None], [None]
        m_wp = None
        wq_free = [None]
        wp_free = [None]

        QK_COLS = [(0, 0, C), (C + 14 * D, C, 2 * D), (C, C + 2 * D, 14 * D)]

        def prep_q(L):
            w = layers[L]
            loads = []
            for src, dst, ncol in QK_COLS:
                loads += w_loads(w["wqkv"], w["bqkv"], src, ncol, dst, 2 * C + dst, 4 * C + dst)
            n, m = stage(loads)
            m_wq[0] = split(n, m, WQ[:, :, :].rearrange("p a n -> p (a n)"),
                            WQL[:, :, :].rearrange("p a n -> p (a n)"), 6 * C, 4 * C, (4 * C, 2 * C), wq_free[0])

        def prep_v(L):
            w = layers[L]
            n, m = stage(w_loads(w["wqkv"], w["bqkv"], 2 * C, C, 0, C, 2 * C))
            m_wv[0] = split(n, m, WV[:, :, :].rearrange("p a n -> p (a n)"),
                            WVL[:, :, :].rearrange("p a n -> p (a n)"), 3 * C, 2 * C, (2 * C, C), wq_free[0])

        def prep_p(L):
            nonlocal m_wp
            w = layers[L]
            n, m = stage(w_loads(w["wo"], w["bo"], 0, C, 0, C, 2 * C))
            m_wp = split(n, m, WP[:, :, :].rearrange("p a n -> p (a n)"),
                         WPL[:, :, :].rearrange("p a n -> p (a n)"), 3 * C, 2 * C, (2 * C, C), wp_free[0])

        pieces = [(0, e, s) for i in range(4) for e in range(NE) for s in range(3)]
        pieces += [(L, 0, s) for L in range(1, 4) for s in range(3)]
        F_FC2, F_C2 = 768, 768 + 3 * C
        m_f = {}
        f_free = [None] * 3
        b2_free = [None] * 2
        m_b2 = {}
        f_n = [0]
        b2s_free = [None]

        def prep_f():
            k = f_n[0]
            if k >= len(pieces):
                return
            f_n[0] += 1
            L, e_, s = pieces[k]
            w = layers[L]
            w1, b1, w2, b2 = w["w1"][e_], w["b1"][e_], w["w2"][e_], w["b2"][e_]
            loads = w_loads(w1, b1, s * 384, 384, 0, 384, F_C2)
            loads.append((lambda t: t[:, F_FC2:F_C2].rearrange("p (j n) -> p j n", j=3),
                          w2[s * 384:(s + 1) * 384, :].rearrange("(j p) n -> p j n", j=3)))
            n, m = stage(loads)
            q = k % 3
            m_f[k] = split(n, m, FH[q][:, :], FL[q][:, :], NSC, NLC, (F_C2, 384), f_free[q])
            if s == 0:
                u = (k // 3) % 2
                mb = sp.do(lambda e, b2=b2: e.dma_start(B2S[:, :], b2.to_broadcast([2, C])), b2s_free[0],
                           sig=s_b2)
                m1 = dve.do(lambda e: e.tensor_copy(r(B2[u][:, :]), B2S[:, :]), mb, b2_free[u])
                m2 = dve.do(lambda e: e.tensor_tensor(r(B2[u][:, :]), B2S[:, :], B2[u][:, :], ALU.subtract), m1)
                m3 = dve.do(lambda e: e.tensor_copy(r(B2[u][0:1, :]), B2S[0:1, :]), m2)
                b2s_free[0] = m3
                m_b2[k // 3] = m3

        m_mf = [None] * 4
        m_gr = [None] * 4
        mf_free = [None] * 2
        gr_free = [None] * 2

        def ada(L):
            w = layers[L]
            marks, gm = [], []
            for j in range(3):
                c0 = j * 2 * C
                n, m = stage([
                    (lambda s: s[:, 0:4 * C].rearrange("p (a n) -> p a n", a=2),
                     w["wada"][0:256, c0:c0 + 2 * C].rearrange("(a p) n -> p a n", a=2)),
                    (lambda s: s[0:32, 4 * C:6 * C], w["wada"][256:288, c0:c0 + 2 * C]),
                    (lambda s: s[32:33, 4 * C:6 * C], w["bada"][:, c0:c0 + 2 * C]),
                ])
                for u in range(2):
                    v = 2 * j + u
                    bk = 6 + v % 2
                    if v in (2, 5):
                        for k in range(3):
                            kk = 128 if k < 2 else 33
                            mm = lambda e, k=k, kk=kk, n=n, u=u, bk=bk: e.matmul(
                                PS[bk][0:4, 0:C], SL[0:kk, k, :],
                                ST[n][0:kk, k * 2 * C + u * C:k * 2 * C + u * C + C],
                                start=(k == 0), stop=(k == 2))
                            mp = pe.do(mm, m, m_sl, bank[bk], end=(k == 2))
                        g = v // 3
                        mg = dve.do(lambda e, g=g, bk=bk: e.tensor_copy(GR[32 * (L % 2):32 * (L % 2) + 4, g, :], PS[bk][0:4, 0:C]),
                                    mp, gr_free[L % 2])
                        bank[bk] = mg
                        gm.append(mg)
                    else:
                        vi = {0: 0, 1: 1, 3: 2, 4: 3}[v]
                        for c, p0, np_ in ((0, 0, 128), (1, 0, 128), (2, 0, 32), (2, 32, 32), (2, 64, 32)):
                            for k in range(3):
                                kk = 128 if k < 2 else 33
                                base = k * 2 * C + u * C + c * 128

                                def mm(e, k=k, kk=kk, n=n, base=base, c=c, bk=bk, p0=p0, np_=np_):
                                    return e.matmul(PS[bk][p0:p0 + np_, 4 * c:4 * c + 4],
                                                    ST[n][0:kk, base:base + np_],
                                                    SL[0:kk, k, :], start=(k == 0), stop=(k == 2))
                                mp = pe.do(mm, m, m_sl, bank[bk], end=(k == 2))
                        add = 1.0 if v in (1, 4) else 0.0

                        def ev(e, vi=vi, bk=bk, add=add, p=128, c0=0, c1=2):
                            return e.tensor_scalar(MF[L % 2][0:p, vi, c0:c1, :],
                                                   PS[bk][0:p, 4 * c0:4 * c1].rearrange("p (c b) -> p c b", b=4),
                                                   add, None, ALU.add)
                        dve.do(ev, mp, mf_free[L % 2])
                        mg = dve.do(lambda e, ev=ev: ev(e, p=96, c0=2, c1=3))
                        bank[bk] = mg
                        marks.append(mg)
                st_free[n] = mp
            m_mf[L], m_gr[L] = marks, gm

        a_free = [None, None]
        a_ready = [k_a[0], k_a[1]]
        xn_free = [None]
        hf_free = [None, None]
        hf_n = [0]
        m_mod_last = [None]

        def rsqrt(m):
            i32 = mybir.dt.int32
            m = dve.do(lambda e: e.tensor_scalar(VV[:, 0, :], MV[:, :, 1], EPS, None, ALU.add), m, rs_free[0])
            m = dve.do(lambda e: e.tensor_scalar(VV[:, 1, :].bitcast(i32), VV[:, 0, :].bitcast(i32), 1, None,
                                                 ALU.logical_shift_right), m)
            m = dve.do(lambda e: e.tensor_scalar(RS[:, :].bitcast(i32), VV[:, 1, :].bitcast(i32),
                                                 -1.0, float(0x5f3759df), ALU.mult, ALU.add), m)
            for _ in range(3):
                m = dve.do(lambda e: e.tensor_tensor(VV[:, 1, :], RS[:, :], RS[:, :], ALU.mult), m)
                m = dve.do(lambda e: e.scalar_tensor_tensor(VV[:, 1, :], VV[:, 1, :], -0.5, VV[:, 0, :],
                                                            ALU.mult, ALU.mult), m)
                m = dve.do(lambda e: e.scalar_tensor_tensor(RS[:, :], VV[:, 1, :], 1.5, RS[:, :],
                                                            ALU.add, ALU.mult), m)
            return m

        rs_free = [None]

        def norm(i, which):
            b = i % 4
            for q in range(QT):
                m1 = dve.do(lambda e, q=q: e.bn_stats(BN[:, q, :], X[:, b * QT + q, :]), m_x[b][q])
                m2 = dve.do(lambda e, q=q: e.bn_aggr(MV[:, q, :], BN[:, q, :]), m1)
            m3 = rsqrt(m2)
            out_ = []
            for q in range(QT):
                dve.do(lambda e, q=q: e.tensor_scalar(
                    XN[:, q, 0:256], X[:, b * QT + q, 0:256], MV[:, q, 0:1], RS[:, q:q + 1],
                    ALU.subtract, ALU.mult), m3, xn_free[0])
                out_.append(dve.do(lambda e, q=q: e.tensor_scalar(
                    XN[:, q, 256:CW_].rearrange("p (a n) -> p a n", a=3),
                    view(X[:, :, :], 0, (b * QT + q) * C + 256, [(1, 128, True), (0, 3, False), (1, 32, False)]),
                    MV[:, q, 0:1], RS[:, q:q + 1], ALU.subtract, ALU.mult)))
            return out_

        def turn(src, m_src, slot, mod, banks):
            a = A[slot]
            done = []
            for c in range(3):
                bk = banks[c % len(banks)]
                np_ = 128 if c < 2 else 96
                for q in range(QT):
                    def tr(e, c=c, q=q, bk=bk):
                        if c < 2:
                            return e.transpose(PS[bk][:, q * 128:(q + 1) * 128],
                                               src[:, q, c * 128:(c + 1) * 128], ID[:, :])
                        return e.transpose(PS[bk][0:96, q * 128:(q + 1) * 128], src[:, q, 256:CW_], ID[:, :])
                    mp = pe.do(tr, m_src[q], k_id, bank[bk], end=(q == QT - 1))
                hi = a[0:np_, [0, 1, 4][c], :]
                if mod is None:
                    mh = act.do(lambda e, bk=bk, hi=hi, np_=np_: e.copy(r(hi), PS[bk][0:np_, :]),
                                mp, a_free[slot], a_ready[slot])
                    full, ready = (lambda p0, p1, bk=bk: PS[bk][p0:p1, :]), mh
                    eng = dve
                else:
                    L, v, b = mod
                    f = hf_n[0] % 2
                    hf_n[0] += 1
                    mfull = act.do(lambda e, bk=bk, f=f, np_=np_, c=c: e.activation(
                        HF[f][0:np_, :], PS[bk][0:np_, :], ACT.Identity,
                        scale=MF[L % 2][0:np_, v + 1, c, b:b + 1], bias=MF[L % 2][0:np_, v, c, b:b + 1]),
                        mp, m_mf[L], hf_free[f])
                    bank[bk] = mfull
                    m_mod_last[0] = mfull
                    mh = dve.do(lambda e, f=f, hi=hi, np_=np_: e.tensor_copy(r(hi), HF[f][0:np_, :]),
                                mfull, a_free[slot], a_ready[slot])
                    full, ready = (lambda p0, p1, f=f: HF[f][p0:p1, :]), mh
                    eng = dve
                if c < 2:
                    ml = eng.do(lambda e, full=full, c=c: e.tensor_tensor(
                        r(a[:, 2 + c, :]), full(0, 128), a[:, c, :], ALU.subtract), ready, a_free[slot])
                else:
                    ml = eng.do(lambda e, full=full: e.tensor_tensor(
                        r(a[32:64, 4, :]), full(32, 64), a[32:64, 4, :], ALU.subtract), ready)
                if mod is None:
                    bank[bk] = ml
                else:
                    hf_free[f] = ml
                done += [mh, ml]
            return done, mp

        def terms(a, wh, wl, wlast, rows=R2):
            return [(a[:, 0, :], wh[0]), (a[:, 1, :], wh[1]), (a[:, 2, :], wh[0]), (a[:, 3, :], wh[1]),
                    (a[:, 0, :], wl[0]), (a[:, 1, :], wl[1]), (a[0:rows, 4, :], wlast[0:rows])]

        QK_TILES = [(0, 7, 0, 0, 7 * D), (0, 7, 1, C + 2 * D, 7 * D), (7, 14, 0, 7 * D, 7 * D),
                    (7, 14, 1, C + 9 * D, 7 * D), (14, 16, None, 14 * D, 4 * D)]
        ks_ready = [k_ks]
        vt_free = [k_vt]
        pb_free = [None] * 3
        stack_free = [None]
        m_qk = {}
        m_v = {}
        m_qt = {}

        def qk_hl(t):
            return view(PB[t // 2][:, :, :], 0, (t % 2) * 2 * T, [(1, 128, True), (T, 2, False), (1, T, False)])

        def qk_out(i, t, f0, row0, nrow):
            tile = view(PB[t // 2][:, :, :], row0, (t % 2) * 2 * T, [(1, nrow, True), (T, 2, False), (1, T, False)])
            return sp.do(lambda e: e.dma_start(
                qkd[i % 2, :, f0:f0 + nrow, :].rearrange("c f n -> f c n"), tile),
                m_qt[t], qkd_free[i % 2], sig=s_qw)

        def qk_in(i, p0, p1, grp, m_w):
            for kind, dst, hls in ((0, QS, (0, 1, 0)), (1, KS, (0, 0, 1))):
                for par in range(2):
                    for blk, hl in enumerate(hls):
                        f0 = kind * C + (2 * p0 + par) * D
                        src = bass.AP(qkd.tensor, qkd.offset + ((i % 2) * 2 + hl) * 2 * C * T + f0 * T,
                                      [[T, D], [2 * D * T, p1 - p0], [1, T]])
                        r0 = 64 * par + blk * D
                        m = sp.do(lambda e, dst=dst, r0=r0, src=src: e.dma_start(dst[r0:r0 + D, p0:p1, :], src),
                                  m_w, stack_free[0], ks_ready[0], sig=s_qk[grp])
            return m

        qkd_free = [None, None]

        def proj_qk(i):
            a = A[0]
            L = i // 4
            for t in range(5):
                bk = 6 + t % 2
                h0, h1, kind, f0, M = QK_TILES[t]

                def cols(w, c, f0=f0, M=M):
                    return w[:, c, f0:f0 + M]
                wh = [cols(WQ, 0), cols(WQ, 1)]
                wl = [cols(WQL, 0), cols(WQL, 1)]
                wlast = cols(WQ, 2)
                tt = terms(a, wh, wl, wlast)
                for n, (x_, w_) in enumerate(tt):
                    mp = pe.do(lambda e, x_=x_, w_=w_, n=n, bk=bk, M=M: e.matmul(
                        PS[bk][0:M, :], r(w_), r(x_), start=(n == 0), stop=(n == 6)),
                        bank[bk], m_a[0], m_wq[0], end=(n == 6))
                hl = qk_hl(t)
                pfree = pb_free[t // 2]
                mh = act.do(lambda e, bk=bk, M=M, hl=hl: e.copy(r(hl[0:M, 0, :]), PS[bk][0:M, :]), mp, pfree)
                ml = dve.do(lambda e, bk=bk, M=M, hl=hl: e.tensor_tensor(
                    r(hl[0:M, 1, :]), PS[bk][0:M, :], hl[0:M, 0, :], ALU.subtract), mh, pfree)
                bank[bk] = ml
                m_qt[t] = [mh, ml]
                if t < 4:
                    mw = qk_out(i, t, kind * C + h0 * D, 0, M)
                else:
                    qk_out(i, t, 14 * D, 0, 2 * D)
                    mw = qk_out(i, t, C + 14 * D, 2 * D, 2 * D)
                if t == 1:
                    m_qk[0] = qk_in(i, 0, 3, 0, mw)
                if t == 4:
                    m_qk[1] = qk_in(i, 3, 8, 1, mw)
                    m_qk["w"] = mw
                    qkd_free[i % 2] = [m_qk[0], m_qk[1]]

        def proj_tok(a, ready, wh, wl, wlast, q, bk, m_w):
            tt = terms(a, wh, wl, wlast)
            for n, (x_, w_) in enumerate(tt):
                mp = pe.do(lambda e, x_=x_, w_=w_, n=n: e.matmul(
                    PS[bk][:, 0:C], r(x_[:, q * 128:(q + 1) * 128]), r(w_), start=(n == 0), stop=(n == 6)),
                    bank[bk], ready, m_w, end=(n == 6))
            return mp

        m_a = [None, None]

        def proj_v(i):
            for q in range(QT):
                bk = 2 + q
                mp = proj_tok(A[0], m_a[0], [WV[:, 0, :], WV[:, 1, :]], [WVL[:, 0, :], WVL[:, 1, :]],
                              WV[:, 2, :], q, bk, m_wv[0])
                m_v[q] = act.do(lambda e, q=q, bk=bk: e.copy(
                    VT[:, q, 0:H * V1].rearrange("p (h d) -> p h d", d=V1)[:, :, 0:D],
                    PS[bk][:, 0:C].rearrange("p (h d) -> p h d", d=D)), mp, vt_free[0])
                bank[bk] = m_v[q]
            a_free[0] = mp
            wq_free[0] = mp

        mx_free = [None, None]
        m2_free = [None, None]
        m_mrow = {}
        m_s1 = [None]

        def s1_steps(i):
            for h in range(H):
                g, hh = h // 4, h % 4
                rb, p = 64 * (h % 2), h // 2
                src = m_qk[0] if h < 6 else m_qk[1]
                for q in range(QT):
                    bk = (h * QT + q) % 2
                    mp = pe.do(lambda e, rb=rb, p=p, q=q, bk=bk: e.matmul(
                        PS[bk][:, :], r(QS[rb:rb + 54, p, q * 128:(q + 1) * 128]), r(KS[rb:rb + 54, p, :]),
                        start=True, stop=True), src, bank[bk])
                    md = dve.do(lambda e, q=q, hh=hh, g=g, bk=bk: e.reduce_max(
                        MX[g % 2][:, 8 * (hh % 2) + 4 * (hh // 2) + q:8 * (hh % 2) + 4 * (hh // 2) + q + 1], PS[bk][:, :], axis=AX.X), mp, mx_free[g % 2])
                    bank[bk] = md
                    if not (hh == 3 and q == 3):
                        yield
                bk = 0
                if hh == 3:
                    mt = pe.do(lambda e, g=g, bk=bk: e.transpose(PS[bk][0:16, 0:128], MX[g % 2][:, :], ID[:, :]),
                               md, bank[bk])
                    mx_free[g % 2] = mt
                    m1 = dve.do(lambda e, g=g, bk=bk: e.tensor_scalar(
                        r(M2[g % 2][:, 0, :]), PS[bk][0:16, 0:128], -1.0, None, ALU.mult), mt, m2_free[0])
                    m2 = dve.do(lambda e, g=g, bk=bk: e.scalar_tensor_tensor(
                        r(M2[g % 2][:, 1, :]), PS[bk][0:16, 0:128], -1.0, M2[g % 2][:, 0, :],
                        ALU.mult, ALU.subtract), m1)
                    bank[bk] = m2
                    for par in range(2):
                        for c in range(2):
                            def go(e, par=par, c=c, g=g):
                                row_ = 64 * par + 54 + c
                                return e.dma_start(
                                    QS[row_:row_ + 1, 2 * g:2 * g + 2, :].rearrange("p a (q n) -> p (a q) n", n=128),
                                    M2[g % 2][8 * par:8 * par + 8, c, :])
                            m_mrow[g] = sp.do(go, m2, stack_free[0], sig=s_m[g])
                    m2_free[0] = m_mrow[g]
                    yield

        os_free = [None]
        ot_free = [None]
        m_ot = [None] * QT
        rd_free = [None]

        def dup_o(m):
            return pool.do(lambda e: e.tensor_copy(
                OT[:, :, C:CW_].rearrange("p q (a n) -> p q a n", a=2),
                view(OT[:, :, :], 0, 256, [(1, 128, True), (CW_, QT, False), (0, 2, False), (1, 32, False)])), m)

        def at_steps(i):
            state = {}

            def s2(st):
                g, kt = st // 4, st % 4
                n = st % 3
                marks = []
                for hh in range(4):
                    h = 4 * g + hh
                    rb, p, bk = 64 * (h % 2), h // 2, 2 + hh
                    mp = pe.do(lambda e, rb=rb, p=p, kt=kt, bk=bk: e.matmul(
                        PS[bk][:, :], r(KS[rb:rb + 56, p, kt * 128:(kt + 1) * 128]), r(QS[rb:rb + 56, p, :]),
                        start=True, stop=True), m_mrow[g], bank[bk])
                    me = act.do(lambda e, n=n, hh=hh, bk=bk: e.activation(
                        PB[n][:, hh, :], PS[bk][:, :], ACT.Exp, scale=SCALE),
                        mp, pb_free[n], m_qk["w"])
                    bank[bk] = me
                    marks.append(me)
                state[st] = marks
                return mp

            def av(st):
                g, kt = st // 4, st % 4
                n = st % 3
                for hh in range(4):
                    h = 4 * g + hh
                    mp = pe.do(lambda e, h=h, hh=hh, kt=kt, n=n: e.matmul(
                        PS[6][32 * hh:32 * hh + 32, :], VT[:, kt, h * V1:h * V1 + 32], PB[n][:, hh, :],
                        start=(kt == 0), stop=(kt == 3)), state[st][hh], m_v[kt], bank[6], end=(hh == 3))
                pb_free[n] = mp
                if kt == 3:
                    mo = act.do(lambda e: e.copy(OS[:, :], PS[6][:, :]), mp, os_free[0])
                    bank[6] = mo
                    state["o", g] = mo
                return mp

            def norm_o(g):
                for q in range(QT):
                    mt = pe.do(lambda e, q=q: e.transpose(
                        PS[7][:, q * 128:(q + 1) * 128], OS[:, q * 128:(q + 1) * 128], ID[:, :]),
                        state["o", g], bank[7], end=(q == QT - 1))
                os_free[0] = mt
                v = PS[7][:, :].rearrange("p (q h d) -> p q h d", q=4, h=4)
                m1 = dve.do(lambda e: e.reciprocal(RD[:, :].rearrange("p (q h) -> p q h", q=4), v[:, :, :, D]),
                            mt, rd_free[0])
                o = OT[:, :, 72 * g:72 * g + 72].rearrange("p q (h d) -> p q h d", d=D)
                m2 = dve.do(lambda e: e.tensor_tensor(
                    o, v[:, :, :, 0:D],
                    view(RD[:, :], 0, 0, [(1, 128, True), (4, 4, False), (1, 4, False), (0, D, False)]),
                    ALU.mult), m1, ot_free[0])
                rd_free[0] = m2
                bank[7] = m2
                return m2

            for st in range(17):
                if st < 16:
                    last = s2(st)
                if st >= 1:
                    mp = av(st - 1)
                if st >= 2 and (st - 2) % 4 == 3:
                    norm_o((st - 2) // 4)
                yield
            stack_free[0] = last
            vt_free[0] = mp
            m_ot[:] = [dup_o(norm_o(3))] * QT
            yield

        pbf = [PB[n][:, :, :].rearrange("p a n -> p (a n)") for n in range(3)]
        l2_tok = [pbf[n][:, 1152:1152 + 3 * C] for n in range(2)]
        l2_mem = [pbf[2][:, 1152:2000], VT[:, :, :].rearrange("p a n -> p (a n)")[:, 0:848]]

        l2 = {"tok": [None, None], "prod": [None] * 4, "S": [None] * 2, "E": [None] * 2, "sm": None, "o": [None] * 2}

        def l2_qkv(i, q):
            dst = l2_tok[q % 2]
            for j in range(3):
                bk = (3 * q + j) % 2
                if j < 2:
                    fs = slice(j * C, (j + 1) * C)
                    mp = proj_tok(A[0], m_a[0], [WQ[:, 0, fs], WQ[:, 1, fs]], [WQL[:, 0, fs], WQL[:, 1, fs]],
                                  WQ[:, 2, fs], q, bk, m_wq[0])
                else:
                    mp = proj_tok(A[0], m_a[0], [WV[:, 0, :], WV[:, 1, :]], [WVL[:, 0, :], WVL[:, 1, :]],
                                  WV[:, 2, :], q, bk, m_wv[0])
                segs = [(0, j * C, C)] if j != 1 else [(0, C + 14 * D, 2 * D), (2 * D, C, 14 * D)]
                for s0, d0, n in segs:
                    me = act.do(lambda e, bk=bk, s0=s0, d0=d0, n=n: e.copy(dst[:, d0:d0 + n], PS[bk][:, s0:s0 + n]),
                                mp, l2["tok"][q % 2], pb_free[q % 2])
                bank[bk] = me
            if q == 3:
                a_free[0] = mp
                wq_free[0] = mp
            return me

        def at2_steps(i):
            b = i % 4
            mq = {}
            mq[0] = l2_qkv(i, 0)
            mq[1] = l2_qkv(i, 1)
            def tile(q):
                tok = l2_tok[q % 2]
                wk = l2_mem[q % 2]
                wk_free = vt_free[0] if q % 2 else pb_free[2]
                S, E, O2, sm = wk[:, 0:256], wk[:, 256:512], wk[:, 512:512 + C], wk[:, 800:848]
                kv_off, vv_off = C, 2 * C
                mr = []
                for u in range(4):
                    pr = pbf[u % 3][:, 0:1152]
                    eng = pool if u == 3 else dve
                    i0 = view(tok, 0, u * 4 * D, [(1, 128, True), (D, 4, False), (0, 16, False), (1, D, False)])
                    i1 = view(tok, 0, kv_off, [(1, 128, True), (0, 4, False), (D, 16, False), (1, D, False)])
                    mpd = eng.do(lambda e, pr=pr, i0=i0, i1=i1: e.tensor_tensor(
                        pr.rearrange("p (h k d) -> p h k d", h=4, k=16), i0, i1, ALU.mult),
                        mq[q], l2["prod"][u % 3], pb_free[u % 3])
                    mr = dve.do(lambda e, pr=pr, u=u: e.tensor_reduce(
                        S[:, u * 64:(u + 1) * 64].rearrange("p (h k) -> p h k", h=4),
                        pr.rearrange("p (h k d) -> p h k d", h=4, k=16), axis=AX.X, op=ALU.add),
                        mpd, l2["S"][q % 2], wk_free)
                    l2["prod"][u % 3] = mr
                    yield
                S3 = S.rearrange("p (h k) -> p h k", h=16)
                E3 = E.rearrange("p (h k) -> p h k", h=16)
                m1 = dve.do(lambda e: e.reduce_max(sm[:, 0:16], S3, axis=AX.X), mr, l2["o"][q % 2])
                m2 = dve.do(lambda e: e.tensor_tensor(
                    S3, S3, view(sm, 0, 0, [(1, 128, True), (1, 16, False), (0, 16, False)]), ALU.subtract), m1)
                m3 = act.do(lambda e: e.activation(E, S, ACT.Exp, scale=SCALE), m2, l2["E"][q % 2])
                m4 = dve.do(lambda e: e.reduce_sum(sm[:, 16:32], E3, axis=AX.X), m3)
                m5 = dve.do(lambda e: e.reciprocal(sm[:, 32:48], sm[:, 16:32]), m4)
                l2["S"][q % 2] = m3
                yield
                for u in range(4):
                    pr = pbf[u % 3][:, 0:1152]
                    eng = pool if u == 3 else dve
                    i0 = view(E, 0, u * 64, [(1, 128, True), (16, 4, False), (0, D, False), (1, 16, False)])
                    i1 = view(tok, 0, vv_off, [(1, 128, True), (0, 4, False), (1, D, False), (D, 16, False)])
                    mpd = eng.do(lambda e, pr=pr, i0=i0, i1=i1: e.tensor_tensor(
                        pr.rearrange("p (h d k) -> p h d k", h=4, d=D), i0, i1, ALU.mult),
                        m3, l2["prod"][u % 3])
                    mr = dve.do(lambda e, pr=pr, u=u: e.tensor_reduce(
                        O2[:, u * 72:(u + 1) * 72].rearrange("p (h d) -> p h d", h=4),
                        pr.rearrange("p (h d k) -> p h d k", h=4, d=D), axis=AX.X, op=ALU.add),
                        mpd, l2["o"][q % 2])
                    l2["prod"][u % 3] = mr
                    yield
                l2["tok"][q % 2] = mr
                l2["E"][q % 2] = mr
                mo = dve.do(lambda e: e.tensor_tensor(
                    O2.rearrange("p (h d) -> p h d", d=D), O2.rearrange("p (h d) -> p h d", d=D),
                    view(sm, 0, 32, [(1, 128, True), (1, 16, False), (0, D, False)]), ALU.mult), mr, m5)
                mw = sp.do(lambda e, O2=O2, q=q: e.dma_start(
                    scr[b, :].rearrange("(h t d) -> t h d", h=H, t=T)[q * 128:(q + 1) * 128],
                    O2.rearrange("p (h d) -> p h d", d=D)), mo, sig=s_sw[q % 2])
                l2["o"][q % 2] = mw
                if q + 2 < QT:
                    mq[q + 2] = l2_qkv(i, q + 2)
                yield
            for q in range(QT):
                yield from tile(q)
            mr = sp.do(lambda e: e.dma_start(
                OT[:, :, 0:C], scr[b, :].rearrange("(q p c) -> p q c", p=128, c=C)),
                l2["o"], ot_free[0], sig=s_sr)
            m_ot[:] = [dup_o(mr)] * QT
            for n in range(3):
                pb_free[n] = [l2["prod"][n], l2["tok"][0], l2["tok"][1], list(l2["o"])]
            if b == 3:
                vt_free[0] = pool.do(lambda e: e.memset(VT[:, :, :], 1.0), l2["tok"][1], list(l2["o"]))
            yield

        gb_free = [None]
        m_gb = [None]

        def gates(i):
            L, b = i // 4, i % 4
            ms = []
            for g in range(2):
                bk = 6 + g
                mp = pe.do(lambda e, g=g, bk=bk: e.matmul(
                    PS[bk][:, 0:C], view(ID[:, :], 32 * (L % 2), 32 * (L % 2) + b, [(1, 4, True), (0, 128, False)]),
                    GR[32 * (L % 2):32 * (L % 2) + 4, g, :], start=True, stop=True), k_id, m_gr[L], bank[bk])
                m = act.do(lambda e, g=g, bk=bk: e.copy(GB[:, g, :], PS[bk][:, 0:C]), mp, gb_free[0])
                bank[bk] = m
                ms.append(m)
            gr_free[L % 2] = mp
            m_gb[0] = ms

        tm_free = [None, None]
        tm_n = [0]

        def residual(i, q, bk, mp, g, scalar=1.0, m_s=None):
            b = i % 4
            u = tm_n[0] % 2
            tm_n[0] += 1
            m1 = dve.do(lambda e: e.scalar_tensor_tensor(
                TM[u][:, :], PS[bk][:, 0:C], scalar, GB[:, g, :], ALU.mult, ALU.mult),
                mp, m_gb[0], m_s, tm_free[u])
            bank[bk] = m1
            m2 = pool.do(lambda e: e.tensor_tensor(
                X[:, b * QT + q, :], X[:, b * QT + q, :], TM[u][:, :], ALU.add), m1, m_x[b][q], xr[b][q])
            tm_free[u] = m2
            m_x[b][q] = m2
            return m1

        xr = [[None] * QT for _ in range(B)]

        def project(i):
            for q in range(QT):
                bk = 2 + q
                mp = proj_tok(A[1], m_a[1], [WP[:, 0, :], WP[:, 1, :]], [WPL[:, 0, :], WPL[:, 1, :]],
                              WP[:, 2, :], q, bk, m_wp)
                residual(i, q, bk, mp, 0)
            a_free[1] = mp
            wp_free[0] = mp

        m_cw = [None]
        cw_free = [None]

        def route(i):
            bk = 6
            for q in range(QT):
                a = A[1]
                tt = terms(a, [WG[:, 0, :], WG[:, 1, :]], [WGL[:, 0, :], WGL[:, 1, :]], WG[:, 2, :], rows=96)
                for n, (x_, w_) in enumerate(tt):
                    mp = pe.do(lambda e, x_=x_, w_=w_, n=n, q=q: e.matmul(
                        PS[bk][:, 4 * q:4 * q + 4], r(x_[:, q * 128:(q + 1) * 128]), r(w_),
                        start=(n == 0), stop=(n == 6)), bank[bk], m_a[1], m_wg, end=(n == 6 and q == QT - 1))
            m = dve.do(lambda e: e.tensor_copy(GL[:, :, :].rearrange("p q e -> p (q e)"), PS[bk][:, 0:16]), mp)
            bank[bk] = m
            mg = m
            m = dve.do(lambda e: e.memset(GK[:, :, :], 0.0))

            def bc(ap, n):
                return view(ap, 0, 0, [(1, 128, True), (4, QT, False), (0, n, False)])
            for j in range(4):
                for lo, hi, op in ((j + 1, 4, ALU.is_ge), (0, j, ALU.is_gt)):
                    if hi <= lo:
                        continue
                    src = view(GL[:, :, :], 0, j, [(1, 128, True), (4, QT, False), (0, hi - lo, False)])
                    m1 = dve.do(lambda e, src=src, lo=lo, hi=hi, op=op: e.tensor_tensor(
                        GC[:, :, lo:hi], src, GL[:, :, lo:hi], op), mg, m)
                    m = dve.do(lambda e, lo=lo, hi=hi: e.tensor_tensor(
                        GK[:, :, lo:hi], GK[:, :, lo:hi], GC[:, :, lo:hi], ALU.add), m1)
            m = dve.do(lambda e: e.tensor_scalar(GK[:, :, :], GK[:, :, :], 1.5, None, ALU.is_lt), m)
            m = dve.do(lambda e: e.reduce_max(GM[:, :], GL[:, :, :], axis=AX.X), m)
            m = dve.do(lambda e: e.tensor_tensor(
                GL[:, :, :], GL[:, :, :], view(GM[:, :], 0, 0, [(1, 128, True), (1, QT, False), (0, 4, False)]),
                ALU.subtract), m)
            m = act.do(lambda e: e.activation(GE[:, :, :], GL[:, :, :], ACT.Exp), m)
            m = dve.do(lambda e: e.tensor_tensor(GE[:, :, :], GE[:, :, :], GK[:, :, :], ALU.mult), m)
            m = dve.do(lambda e: e.reduce_sum(GS[:, :], GE[:, :, :], axis=AX.X), m)
            m = dve.do(lambda e: e.reciprocal(GM[:, :], GS[:, :]), m)
            m_cw[0] = dve.do(lambda e: e.tensor_tensor(
                CW[:, :, :], GE[:, :, :], view(GM[:, :], 0, 0, [(1, 128, True), (1, QT, False), (0, 4, False)]),
                ALU.mult), m, cw_free[0])

        hh_free = [None] * 3
        hh_n = [0]

        def ffn_steps(i):
            L, b = i // 4, i % 4
            func = ACT.Gelu if L == 2 else ACT.Gelu_apprx_tanh
            a = A[1]
            for e_ in range(NE if L == 0 else 1):
                k0 = (i * NE + e_) * 3 if L == 0 else 48 + (L - 1) * 3
                last_use = L == 0 or b == 3
                hid = {}

                def fc1(j):
                    k, jj = k0 + j // 3, j % 3
                    q = k % 3
                    bk = 6 + j % 2
                    wh = [FH[q][:, c * 384 + jj * 128:c * 384 + jj * 128 + 128] for c in range(2)]
                    wl = [FL[q][:, c * 384 + jj * 128:c * 384 + jj * 128 + 128] for c in range(2)]
                    wlast = FH[q][:, F_C2 + jj * 128:F_C2 + jj * 128 + 128]
                    for n, (x_, w_) in enumerate(terms(a, wh, wl, wlast)):
                        mp = pe.do(lambda e, x_=x_, w_=w_, n=n, bk=bk: e.matmul(
                            PS[bk][:, :], r(w_), r(x_), start=(n == 0), stop=(n == 6)),
                            bank[bk], m_a[1], m_f[k], end=(n == 6))
                    f = hf_n[0] % 2
                    hf_n[0] += 1
                    u = hh_n[0] % 3
                    hh_n[0] += 1
                    mg = act.do(lambda e, f=f, bk=bk: e.activation(HF[f][:, :], PS[bk][:, :], func),
                                mp, hf_free[f])
                    bank[bk] = mg
                    mh = dve.do(lambda e, f=f, u=u: e.tensor_copy(r(HH[u][:, 0, :]), HF[f][:, :]), mg, hh_free[u])
                    ml = dve.do(lambda e, f=f, u=u: e.tensor_tensor(
                        r(HH[u][:, 1, :]), HF[f][:, :], HH[u][:, 0, :], ALU.subtract), mh)
                    hf_free[f] = ml
                    hid[j] = (u, [mh, ml])
                    return mp

                def fc2(j):
                    k, jj = k0 + j // 3, j % 3
                    q = k % 3
                    u, ready = hid[j]
                    c0 = F_FC2 + jj * C
                    wh, wl = FH[q][:, c0:c0 + C], FL[q][:, c0:c0 + C]
                    for t in range(QT):
                        tk = slice(t * 128, (t + 1) * 128)
                        if j == 0:
                            pe.do(lambda e, t=t: e.matmul(PS[2 + t][:, 0:C], r(ON[:, :]), r(B2[(k // 3) % 2][:, :]),
                                                          start=True, stop=False),
                                  bank[2 + t], m_b2[k // 3], k_on, end=False)
                        for n, (c, w_) in enumerate(((0, wh), (1, wh), (0, wl))):
                            mp = pe.do(lambda e, t=t, tk=tk, c=c, w_=w_, n=n: e.matmul(
                                PS[2 + t][:, 0:C], r(HH[u][:, c, tk]), r(w_), start=False,
                                stop=(j == NCH - 1 and n == 2)), ready,
                                end=(n == 2 and (j == NCH - 1 or t == QT - 1)))
                        if j == NCH - 1:
                            if L == 0:
                                residual(i, t, 2 + t, mp, 1, CW[:, t, e_:e_ + 1], m_cw[0])
                            else:
                                residual(i, t, 2 + t, mp, 1)
                    hh_free[u] = mp
                    if jj == 2 and last_use:
                        f_free[q] = mp
                        if j == NCH - 1:
                            b2_free[(k // 3) % 2] = mp
                        todo.append(1)
                    return mp

                todo = []
                for j in range(NCH + 1):
                    if j < NCH:
                        m1 = fc1(j)
                        if j == NCH - 1:
                            a_last = m1
                    if todo:
                        todo.pop()
                        prep_f()
                    if j >= 1:
                        fc2(j - 1)
                    yield
                if todo:
                    prep_f()
            a_free[1] = a_last
            cw_free[0] = (s_dve, s_dve.n)
            gb_free[0] = (s_dve, s_dve.n)

        def drain(gen):
            for _ in gen:
                pass

        def weave(main, side, ratio):
            acc = 0.0
            for _ in main:
                acc += ratio
                while acc >= 1 and side is not None:
                    acc -= 1
                    if next(side, "end") == "end":
                        side = None
            return side

        load_x(0)
        ada(0)
        prep_q(0)
        prep_v(0)
        n, m = stage([
            (lambda s: s[:, 0:8].rearrange("p (a n) -> p a n", a=2),
             gate_w[0:256, :].rearrange("(a p) n -> p a n", a=2)),
            (lambda s: s[0:96, 8:12], gate_w[256:288, :].unsqueeze(0).to_broadcast([3, 32, 4])),
        ])
        m_wg = split(n, m, WG[:, :, :].rearrange("p a n -> p (a n)"), WGL[:, :, :].rearrange("p a n -> p (a n)"),
                     12, 8, (8, 4), None)
        for b in range(1, B):
            load_x(b)

        def front(i):
            mn = norm(i, 0)
            done, mp = turn(XN, mn, 0, (i // 4, 0, i % 4), [7])
            m_a[0] = done
            xn_free[0] = mp

        front(0)
        prep_p(0)
        for _ in range(3):
            prep_f()

        def start_att(i):
            if i // 4 == 2:
                return None, at2_steps(i)
            proj_qk(i)
            proj_v(i)
            return s1_steps(i), at_steps(i)

        s1, at = start_att(0)
        for i in range(NI):
            L, b = i // 4, i % 4
            gates(i)
            if L == 2:
                drain(at)
                if i + 1 < NI:
                    if b == 3:
                        prep_q(L + 1)
                        prep_v(L + 1)
                    front(i + 1)
            else:
                drained = s1
                if drained is not None:
                    drain(drained)
                for n, _ in enumerate(at):
                    if n == 4 and i + 1 < NI:
                        front(i + 1)
            if b == 2 and L < 3:
                ada(L + 1)
            done, mp = turn(OT, m_ot, 1, None, [7])
            m_a[1] = done
            ot_free[0] = mp
            project(i)
            if b == 3 and L < 3:
                prep_p(L + 1)
            if i + 1 < NI:
                s1n, atn = start_att(i + 1)
            else:
                s1n, atn = None, None
            mn = norm(i, 1)
            done, mp = turn(XN, mn, 1, (L, 2, b), [7])
            m_a[1] = done
            xn_free[0] = mp
            mf_free[L % 2] = m_mod_last[0]
            if L == 0:
                route(i)
            if b == 2 and L < 3 and L != 2:
                prep_q(L + 1)
                prep_v(L + 1)
            steps = 10 * (NE if L == 0 else 1)
            ratio = (64.0 if L == 0 else 40.0) / steps
            if s1n is not None:
                s1 = weave(ffn_steps(i), s1n, ratio)
            elif atn is not None:
                side = weave(ffn_steps(i), atn, 2.0)
                s1 = None
                atn = side if side is not None else iter(())
            else:
                drain(ffn_steps(i))
                s1 = None
            at = atn
            if L == 3:
                o_v = out.rearrange("b (q p) c -> b p q c", p=128)
                mo = sp.do(lambda e, b=b: e.dma_start(o_v[b], X[:, b * QT:(b + 1) * QT, :]), m_x[b], sig=s_out)
        sp.wait(mo)
        for s in s_sw:
            sp.wait((s, s.n))
        sp.wait((s_qw, s_qw.n))

        block = ctx.enter_context(nc.Block())

        @block.sync
        def _(e):
            sp.run(e)

        @block.gpsimd
        def _(e):
            pool.run(e)

        @block.scalar
        def _(e):
            act.run(e)

        @block.vector
        def _(e):
            dve.run(e)

        @block.tensor
        def _(e):
            pe.run(e)


_NAMES = [
    ("L0_cond_", ["w_adaln", "b_adaln", "w_qkv", "b_qkv", "w_proj", "b_proj", "w1", "b1", "w2", "b2"]),
    ("L1_cond_", ["W_ada", "b_ada", "W_qkv", "b_qkv", "W_proj", "b_proj", "W_fc1", "b_fc1", "W_fc2", "b_fc2"]),
    ("L2_cond_", ["ada_w", "ada_b", "qkv_w", "qkv_b", "proj_w", "proj_b", "fc1_w", "fc1_b", "fc2_w", "fc2_b"]),
    ("L3_cond_", ["ada_w", "ada_b", "qkv_w", "qkv_b", "out_w", "out_b", "w1", "b1", "w2", "b2"]),
]


def kernel(**inputs):
    import concourse.bacc as bacc
    from concourse.bass_utils import run_bass_kernel_spmd as run

    nc = bacc.Bacc("TRN2", target_bir_lowering=False, num_devices=1, dynamic_dma_scratch_size=1024)
    arrays = {}

    def arg(name):
        a = np.ascontiguousarray(inputs[name])
        arrays["in_" + name] = a
        return nc.dram_tensor("in_" + name, a.shape, mybir.dt.from_np(a.dtype), kind="ExternalInput").ap()

    def row(ap):
        return ap.rearrange("(a n) -> a n", a=1)

    x, cond = arg("x"), arg("cond_1152")
    layers = []
    for n, (pre, names) in enumerate(_NAMES):
        a = [arg(pre + s) for s in names]
        if n == 0:
            w1 = [a[6][e] for e in range(NE)]
            b1 = [a[7][e:e + 1, :] for e in range(NE)]
            w2 = [a[8][e] for e in range(NE)]
            b2 = [a[9][e:e + 1, :] for e in range(NE)]
        else:
            w1, b1, w2, b2 = [a[6]], [row(a[7])], [a[8]], [row(a[9])]
        layers.append({"wada": a[0], "bada": row(a[1]), "wqkv": a[2], "bqkv": row(a[3]), "wo": a[4],
                       "bo": row(a[5]), "w1": w1, "b1": b1, "w2": w2, "b2": b2})
    gate_w = arg("L0_cond_w_gate")
    out = nc.dram_tensor("out_0", (B, T, C), F32, kind="ExternalOutput").ap()
    build(nc, x, cond, layers, gate_w, out)
    res = run(nc, [arrays], core_ids=[0])
    return res.results[0]["out_0"]
```

```python
import numpy as np
import concourse.bass as bass
from concourse import mybir
from contextlib import ExitStack

F32 = mybir.dt.float32
F32R = mybir.dt.float32r
ALU = mybir.AluOpType
ACT = mybir.ActivationFunctionType
AX = mybir.AxisListType

B, T, C, H, D = 4, 512, 288, 16, 18
QT = T // 128
NI = 16
NE = 4
NCH = 9
V1 = D + 1
SCALE = float(D) ** -0.5
EPS = 1e-6
R2 = 98
CW_ = 256 + 3 * 32
MID = 2.0
RATIO = (1.2, 3.5, 2.0)


def r(ap):
    return ap.bitcast(F32R)


def view(ap, part, free, dims):
    step = ap.ap[0][0]
    return bass.AP(ap.tensor, ap.offset + part * step + free,
                   [[s * step if isp else s, n] for s, n, isp in dims])


class Count:

    def __init__(self, sem, step=1):
        self.sem, self.step, self.n = sem, step, 0


class Queue:

    def __init__(self, done=None):
        self.items, self.seen, self.done = [], {}, done

    def wait(self, *marks):
        for m in marks:
            if m is None:
                continue
            if isinstance(m, list):
                self.wait(*m)
                continue
            c, v = m
            if self.seen.get(id(c), 0) < v:
                self.seen[id(c)] = v
                self.items.append(lambda e, c=c, v=v: e.wait_ge(c.sem, v))

    def do(self, fn, *marks, sig=None, end=True):
        self.wait(*marks)
        if not end:
            self.items.append(fn)
            return None
        c = sig or self.done
        c.n += c.step
        self.items.append(lambda e: fn(e).then_inc(c.sem, c.step))
        return (c, c.n)

    def run(self, e):
        for f in self.items:
            f(e)


def build(nc, x_in, cond, layers, gate_w, out):
    ctx = ExitStack()
    with ctx:
        def sb(name, shape):
            return ctx.enter_context(nc.sbuf_tensor(name, shape, F32))

        def sem(name, step=1):
            return Count(ctx.enter_context(nc.semaphore(name)), step)

        X = sb("X", [128, B * QT, C])
        A = [sb(f"A{n}", [128, 5, T]) for n in range(2)]
        WQ = sb("WQ", [128, 3, 2 * C])
        WQL = sb("WQL", [128, 2, 2 * C])
        WV = sb("WV", [128, 3, C])
        WVL = sb("WVL", [128, 2, C])
        WP = sb("WP", [128, 3, C])
        WPL = sb("WPL", [128, 2, C])
        NSC = 3 * (3 * 128) + 3 * C
        NLC = 2 * (3 * 128) + 3 * C
        FH = [sb(f"FH{n}", [128, NSC]) for n in range(3)]
        FL = [sb(f"FL{n}", [128, NLC]) for n in range(3)]
        ST = [sb(f"ST{n}", [128, NSC]) for n in range(2)]
        B2 = [sb(f"B2{n}", [2, C]) for n in range(2)]
        B2S = sb("B2S", [2, C])
        HF = [sb(f"HF{n}", [128, T]) for n in range(2)]
        HH = [sb(f"HH{n}", [128, 2, T]) for n in range(3)]
        QS = sb("QS", [128, 8, T])
        KS = sb("KS", [128, 8, T])
        VT = sb("VT", [128, QT, H * V1 + 13])
        PB = [sb(f"PB{n}", [128, 4, T]) for n in range(3)]
        OT = sb("OT", [128, QT, CW_])
        XN = sb("XN", [128, QT, CW_])
        TM = [sb(f"TM{n}", [128, C]) for n in range(2)]
        GB = sb("GB", [128, 2, C])
        GR = sb("GR", [36, 2, C])
        MF = [sb(f"MF{n}", [128, 4, 3, 4]) for n in range(2)]
        ID = sb("ID", [128, 128])
        ON = sb("ON", [2, 128])
        CT = sb("CT", [128, 3, 4])
        SL = sb("SL", [128, 3, 4])
        BN = sb("BN", [128, QT, 6])
        MV = sb("MV", [128, QT, 2])
        RS = sb("RS", [128, QT])
        VV = sb("VV", [128, 2, QT])
        OS = sb("OS", [128, T])
        MX = [sb(f"MX{n}", [128, 16]) for n in range(2)]
        M2 = [sb("M2", [16, 2, 128])] * 2
        RD = sb("RD", [128, 16])
        WG = sb("WG", [128, 3, 4])
        WGL = sb("WGL", [128, 2, 4])
        GL = sb("GL", [128, QT, 4])
        GK = sb("GK", [128, QT, 4])
        GC = sb("GC", [128, QT, 4])
        GE = sb("GE", [128, QT, 4])
        CW = sb("CW", [128, QT, 4])
        GM = sb("GM", [128, QT])
        GS = sb("GS", [128, QT])
        PS = [ctx.enter_context(nc.psum_tensor(f"PS{n}", [128, 512], F32)) for n in range(8)]
        qkd = nc.dram_tensor("qkd", [2, 2, 2 * C, T], F32, kind="Internal").ap()
        scr = nc.dram_tensor("scr", [B, H * T * D], F32, kind="Internal").ap()

        s_pe, s_act, s_dve, s_pool = sem("s_pe"), sem("s_act"), sem("s_dve"), sem("s_pool")
        s_x = [sem(f"s_x{b}", 16) for b in range(B)]
        s_c = sem("s_c", 16)
        s_g = sem("s_g", 16)
        s_st = [sem(f"s_st{n}", 16) for n in range(2)]
        s_b2 = sem("s_b2", 16)
        s_qk = [sem(f"s_qk{n}", 16) for n in range(3)]
        s_qw = [sem(f"s_qw{n}", 16) for n in range(3)]
        s_m = [sem(f"s_m{n}", 16) for n in range(4)]
        s_sw = [sem(f"s_sw{n}", 16) for n in range(2)]
        s_sr = sem("s_sr", 16)
        s_out = sem("s_out", 16)

        pe, act, dve, pool, sp = Queue(s_pe), Queue(s_act), Queue(s_dve), Queue(s_pool), Queue()

        bank = [None] * 8

        m = pool.do(lambda e: e.memset(ID[:, :], 0.0))
        k_id = pool.do(lambda e: e.affine_select(out=ID[:, :], in_=ID[:, :], compare_op=ALU.not_equal,
                                                 fill=1.0, base=0, pattern=[[-1, 128]],
                                                 channel_multiplier=1), m)
        k_on = pool.do(lambda e: e.memset(ON[:, :], 1.0))
        k_st = [pool.do(lambda e, n=n: e.memset(ST[n][:, :], 0.0)) for n in range(2)]
        k_ct = pool.do(lambda e: e.memset(CT[:, :, :], 0.0))
        k_sl = pool.do(lambda e: e.memset(SL[:, :, :], 1.0))
        k_a = [pool.do(lambda e, n=n: e.memset(A[n][:, 4, :], 1.0)) for n in range(2)]
        k_ks = pool.do(lambda e: e.memset(KS[:, :, :], 1.0))
        k_vt = pool.do(lambda e: e.memset(VT[:, :, :], 1.0))

        m_c = None
        for c in range(3):
            n = 128 if c < 2 else 32
            m_c = sp.do(lambda e, c=c, n=n: e.dma_start(
                CT[0:n, c, :], cond[:, c * 128:c * 128 + n].rearrange("b k -> k b"),
                allow_slow_non_contiguous=True), k_ct, sig=s_c)
        m_sl = act.do(lambda e: e.activation(SL[:, 0:2, :], CT[:, 0:2, :], ACT.Silu), m_c, k_sl)
        m_sl = act.do(lambda e: e.activation(SL[0:32, 2, :], CT[0:32, 2, :], ACT.Silu))
        x_v = x_in.rearrange("b (q p) c -> b p q c", p=128)
        m_x = [None] * B

        def load_x(b):
            m = sp.do(lambda e, b=b: e.dma_start(X[:, b * QT:(b + 1) * QT, :], x_v[b]), sig=s_x[b])
            m_x[b] = [m] * QT

        st_n = [0]
        st_free = [k_st[0], k_st[1]]

        jobs = [("ada", 0, j) for j in range(3)] + [("q", 0), ("v", 0), ("wg",), ("p", 0)]
        jobs += [("f", k) for k in range(3)]
        k_ = 3
        for i_ in range(NI):
            L_, b_ = i_ // 4, i_ % 4
            if L_ < 3:
                if b_ == 1:
                    jobs += [("ada", L_ + 1, j) for j in range(3)]
                if b_ == (3 if L_ == 2 else 2):
                    jobs += [("q", L_ + 1), ("v", L_ + 1)]
                if b_ == 3:
                    jobs += [("p", L_ + 1)]
            if L_ == 0 or b_ == 3:
                n_ = min(3 * NE if L_ == 0 else 3, 4 * NE * 3 + 9 - k_)
                jobs += [("f", k) for k in range(k_, k_ + n_)]
                k_ += n_
        job_mark = {}

        def ahead():
            k = len(job_mark)
            if k >= len(jobs) or k >= st_n[0] + 2:
                return
            n = k % 2
            for dst, src in loads_of(jobs[k]):
                m = sp.do(lambda e, dst=dst, src=src, n=n: e.dma_start(dst(ST[n]), src),
                          st_free[n], sig=s_st[n])
            job_mark[k] = m

        def stage(key):
            k = st_n[0]
            assert jobs[k] == key, (jobs[k], key)
            if k not in job_mark:
                ahead()
            st_n[0] += 1
            return k % 2, job_mark[k]

        def loads_of(key):
            kind = key[0]
            if kind == "wg":
                return [
                    (lambda s: s[:, 0:8].rearrange("p (a n) -> p a n", a=2),
                     gate_w[0:256, :].rearrange("(a p) n -> p a n", a=2)),
                    (lambda s: s[0:96, 8:12], gate_w[256:288, :].unsqueeze(0).to_broadcast([3, 32, 4])),
                ]
            if kind == "f":
                L, e_, s_ = pieces[key[1]]
                w = layers[L]
                loads = w_loads(w["w1"][e_], w["b1"][e_], s_ * 384, 384, 0, 384, F_C2)
                loads.append((lambda t: t[:, F_FC2:F_C2].rearrange("p (j n) -> p j n", j=3),
                              w["w2"][e_][s_ * 384:(s_ + 1) * 384, :].rearrange("(j p) n -> p j n", j=3)))
                return loads
            w = layers[key[1]]
            if kind == "q":
                loads = []
                for src, dst, ncol in QK_COLS:
                    loads += w_loads(w["wqkv"], w["bqkv"], src, ncol, dst, 2 * C + dst, 4 * C + dst)
                return loads
            if kind == "v":
                return w_loads(w["wqkv"], w["bqkv"], 2 * C, C, 0, C, 2 * C)
            if kind == "p":
                return w_loads(w["wo"], w["bo"], 0, C, 0, C, 2 * C)
            c0 = key[2] * 2 * C
            return [
                (lambda s: s[:, 0:4 * C].rearrange("p (a n) -> p a n", a=2),
                 w["wada"][0:256, c0:c0 + 2 * C].rearrange("(a p) n -> p a n", a=2)),
                (lambda s: s[0:32, 4 * C:6 * C], w["wada"][256:288, c0:c0 + 2 * C]),
                (lambda s: s[32:33, 4 * C:6 * C], w["bada"][:, c0:c0 + 2 * C]),
            ]

        def w_loads(w, bias, c0, ncol, o0, o1, o2):
            def two(s):
                return view(s[:, :], 0, o0, [(1, 128, True), (o1 - o0, 2, False), (1, ncol, False)])
            return [
                (two, w[0:256, c0:c0 + ncol].rearrange("(a p) n -> p a n", a=2)),
                (lambda s: s[0:96, o2:o2 + ncol],
                 w[256:288, c0:c0 + ncol].unsqueeze(0).to_broadcast([3, 32, ncol])),
                (lambda s: s[96:98, o2:o2 + ncol],
                 bias[:, c0:c0 + ncol].to_broadcast([2, ncol])),
            ]

        def split(key, hi, lo, nh, nl, fix, free, done):
            n, m_ld = stage(key)
            mh = dve.do(lambda e: e.tensor_copy(r(hi), ST[n][:, 0:nh]), m_ld, free())
            ml = pool.do(lambda e: e.tensor_tensor(r(lo), ST[n][:, 0:nl], hi[:, 0:nl], ALU.subtract), mh, free())
            yield
            f0, nf = fix
            m1 = dve.do(lambda e: e.tensor_tensor(r(hi[64:R2, f0:f0 + nf]), ST[n][64:R2, f0:f0 + nf],
                                                  hi[64:R2, f0:f0 + nf], ALU.subtract), mh)
            m2 = dve.do(lambda e: e.tensor_copy(r(hi[96:97, f0:f0 + nf]), ST[n][96:97, f0:f0 + nf]), m1)
            st_free[n] = [ml, m2]
            done([ml, m2])
            yield
            ahead()
            yield

        m_wq, m_wv = [None], [None]
        m_wp = [None]
        wq_free = [None]
        wp_free = [None]

        QK_COLS = [(0, 0, C), (C + 14 * D, C, 2 * D), (C, C + 2 * D, 14 * D)]

        def flat(ap):
            return ap[:, :, :].rearrange("p a n -> p (a n)")

        def prep_q(L):
            yield from split(("q", L), flat(WQ), flat(WQL), 6 * C, 4 * C, (4 * C, 2 * C), lambda: wq_free[0],
                             lambda m: m_wq.__setitem__(0, m))

        def prep_v(L):
            yield from split(("v", L), flat(WV), flat(WVL), 3 * C, 2 * C, (2 * C, C), lambda: wq_free[0],
                             lambda m: m_wv.__setitem__(0, m))

        def prep_p(L):
            yield from split(("p", L), flat(WP), flat(WPL), 3 * C, 2 * C, (2 * C, C), lambda: wp_free[0],
                             lambda m: m_wp.__setitem__(0, m))

        pieces = [(0, e, s) for i in range(4) for e in range(NE) for s in range(3)]
        pieces += [(L, 0, s) for L in range(1, 4) for s in range(3)]
        F_FC2, F_C2 = 768, 768 + 3 * C
        m_f = {}
        f_free = [None] * 3
        b2_free = [None] * 2
        m_b2 = {}
        f_n = [0]
        b2s_free = [None]

        def prep_f():
            k = f_n[0]
            if k >= len(pieces):
                return
            f_n[0] += 1
            L, e_, s_ = pieces[k]
            q = k % 3
            if s_ == 0:
                mb = sp.do(lambda e: e.dma_start(B2S[:, :], layers[L]["b2"][e_].to_broadcast([2, C])),
                           b2s_free[0], sig=s_b2)
            yield from split(("f", k), FH[q][:, :], FL[q][:, :], NSC, NLC, (F_C2, 384), lambda: f_free[q],
                             lambda m: m_f.__setitem__(k, m))
            if s_ == 0:
                u = (k // 3) % 2
                m1 = dve.do(lambda e: e.tensor_copy(r(B2[u][:, :]), B2S[:, :]), mb, b2_free[u])
                m2 = dve.do(lambda e: e.tensor_tensor(r(B2[u][:, :]), B2S[:, :], B2[u][:, :], ALU.subtract), m1)
                m3 = dve.do(lambda e: e.tensor_copy(r(B2[u][0:1, :]), B2S[0:1, :]), m2)
                b2s_free[0] = m3
                m_b2[k // 3] = m3
                yield

        m_mf = [None] * 4
        m_gr = [None] * 4
        mf_free = [None] * 2
        gr_free = [None] * 2

        def ada(L):
            marks, gm = [], []
            for j in range(3):
                n, m = stage(("ada", L, j))
                for u in range(2):
                    v = 2 * j + u
                    bk = 6 + v % 2
                    if v in (2, 5):
                        for k in range(3):
                            kk = 128 if k < 2 else 33
                            mm = lambda e, k=k, kk=kk, n=n, u=u, bk=bk: e.matmul(
                                PS[bk][0:4, 0:C], SL[0:kk, k, :],
                                ST[n][0:kk, k * 2 * C + u * C:k * 2 * C + u * C + C],
                                start=(k == 0), stop=(k == 2))
                            mp = pe.do(mm, m, m_sl, bank[bk], end=(k == 2))
                        g = v // 3
                        mg = dve.do(lambda e, g=g, bk=bk: e.tensor_copy(GR[32 * (L % 2):32 * (L % 2) + 4, g, :], PS[bk][0:4, 0:C]),
                                    mp, gr_free[L % 2])
                        bank[bk] = mg
                        gm.append(mg)
                    else:
                        vi = {0: 0, 1: 1, 3: 2, 4: 3}[v]
                        for c, p0, np_ in ((0, 0, 128), (1, 0, 128), (2, 0, 32), (2, 32, 32), (2, 64, 32)):
                            for k in range(3):
                                kk = 128 if k < 2 else 33
                                base = k * 2 * C + u * C + c * 128

                                def mm(e, k=k, kk=kk, n=n, base=base, c=c, bk=bk, p0=p0, np_=np_):
                                    return e.matmul(PS[bk][p0:p0 + np_, 4 * c:4 * c + 4],
                                                    ST[n][0:kk, base:base + np_],
                                                    SL[0:kk, k, :], start=(k == 0), stop=(k == 2))
                                mp = pe.do(mm, m, m_sl, bank[bk], end=(k == 2))
                        add = 1.0 if v in (1, 4) else 0.0

                        def ev(e, vi=vi, bk=bk, add=add, p=128, c0=0, c1=2):
                            return e.tensor_scalar(MF[L % 2][0:p, vi, c0:c1, :],
                                                   PS[bk][0:p, 4 * c0:4 * c1].rearrange("p (c b) -> p c b", b=4),
                                                   add, None, ALU.add)
                        dve.do(ev, mp, mf_free[L % 2])
                        mg = dve.do(lambda e, ev=ev: ev(e, p=96, c0=2, c1=3))
                        bank[bk] = mg
                        marks.append(mg)
                    yield
                st_free[n] = mp
                ahead()
                yield
            m_mf[L], m_gr[L] = marks, gm

        a_free = [None, None]
        m_a = [None, None]
        a_ready = [k_a[0], k_a[1]]
        xn_free = [None]
        hf_free = [None, None]
        hf_n = [0]
        m_mod_last = [None]

        def rsqrt(m):
            i32 = mybir.dt.int32
            m = dve.do(lambda e: e.tensor_scalar(VV[:, 0, :], MV[:, :, 1], EPS, None, ALU.add), m, rs_free[0])
            m = dve.do(lambda e: e.tensor_scalar(VV[:, 1, :].bitcast(i32), VV[:, 0, :].bitcast(i32), 1, None,
                                                 ALU.logical_shift_right), m)
            m = dve.do(lambda e: e.tensor_scalar(RS[:, :].bitcast(i32), VV[:, 1, :].bitcast(i32),
                                                 -1.0, float(0x5f3759df), ALU.mult, ALU.add), m)
            for _ in range(3):
                m = dve.do(lambda e: e.tensor_tensor(VV[:, 1, :], RS[:, :], RS[:, :], ALU.mult), m)
                m = dve.do(lambda e: e.scalar_tensor_tensor(VV[:, 1, :], VV[:, 1, :], -0.5, VV[:, 0, :],
                                                            ALU.mult, ALU.mult), m)
                m = dve.do(lambda e: e.scalar_tensor_tensor(RS[:, :], VV[:, 1, :], 1.5, RS[:, :],
                                                            ALU.add, ALU.mult), m)
            return m

        rs_free = [None]

        def norm(i, which):
            b = i % 4
            for q in range(QT):
                m1 = dve.do(lambda e, q=q: e.bn_stats(BN[:, q, :], X[:, b * QT + q, :]), m_x[b][q])
                m2 = dve.do(lambda e, q=q: e.bn_aggr(MV[:, q, :], BN[:, q, :]), m1)
            m3 = rsqrt(m2)
            out_ = []
            for q in range(QT):
                dve.do(lambda e, q=q: e.tensor_scalar(
                    XN[:, q, 0:256], X[:, b * QT + q, 0:256], MV[:, q, 0:1], RS[:, q:q + 1],
                    ALU.subtract, ALU.mult), m3, xn_free[0])
                out_.append(dve.do(lambda e, q=q: e.tensor_scalar(
                    XN[:, q, 256:CW_].rearrange("p (a n) -> p a n", a=3),
                    view(X[:, :, :], 0, (b * QT + q) * C + 256, [(1, 128, True), (0, 3, False), (1, 32, False)]),
                    MV[:, q, 0:1], RS[:, q:q + 1], ALU.subtract, ALU.mult)))
            return out_

        def turn(src, m_src, slot, mod, banks):
            a = A[slot]
            m_a[slot] = done = []
            for c in range(3):
                bk = banks[c % len(banks)]
                np_ = 128 if c < 2 else 96
                for q in range(QT):
                    def tr(e, c=c, q=q, bk=bk):
                        if c < 2:
                            return e.transpose(PS[bk][:, q * 128:(q + 1) * 128],
                                               src[:, q, c * 128:(c + 1) * 128], ID[:, :])
                        return e.transpose(PS[bk][0:96, q * 128:(q + 1) * 128], src[:, q, 256:CW_], ID[:, :])
                    mp = pe.do(tr, m_src[q], k_id, bank[bk], end=(q == QT - 1))
                hi = a[0:np_, [0, 1, 4][c], :]
                if mod is None:
                    mh = act.do(lambda e, bk=bk, hi=hi, np_=np_: e.copy(r(hi), PS[bk][0:np_, :]),
                                mp, a_free[slot], a_ready[slot])
                    full, ready = (lambda p0, p1, bk=bk: PS[bk][p0:p1, :]), mh
                    eng = dve
                else:
                    L, v, b = mod
                    f = hf_n[0] % 2
                    hf_n[0] += 1
                    mfull = act.do(lambda e, bk=bk, f=f, np_=np_, c=c: e.activation(
                        HF[f][0:np_, :], PS[bk][0:np_, :], ACT.Identity,
                        scale=MF[L % 2][0:np_, v + 1, c, b:b + 1], bias=MF[L % 2][0:np_, v, c, b:b + 1]),
                        mp, m_mf[L], hf_free[f])
                    bank[bk] = mfull
                    m_mod_last[0] = mfull
                    mh = dve.do(lambda e, f=f, hi=hi, np_=np_: e.tensor_copy(r(hi), HF[f][0:np_, :]),
                                mfull, a_free[slot], a_ready[slot])
                    full, ready = (lambda p0, p1, f=f: HF[f][p0:p1, :]), mh
                    eng = dve
                if c < 2:
                    ml = eng.do(lambda e, full=full, c=c: e.tensor_tensor(
                        r(a[:, 2 + c, :]), full(0, 128), a[:, c, :], ALU.subtract), ready, a_free[slot])
                else:
                    ml = eng.do(lambda e, full=full: e.tensor_tensor(
                        r(a[32:64, 4, :]), full(32, 64), a[32:64, 4, :], ALU.subtract), ready)
                if mod is None:
                    bank[bk] = ml
                else:
                    hf_free[f] = ml
                done += [mh, ml]
                yield
            return mp

        def terms(a, wh, wl, wlast, rows=R2):
            return [(a[:, 0, :], wh[0]), (a[:, 1, :], wh[1]), (a[:, 2, :], wh[0]), (a[:, 3, :], wh[1]),
                    (a[:, 0, :], wl[0]), (a[:, 1, :], wl[1]), (a[0:rows, 4, :], wlast[0:rows])]

        QK_TILES = [(0, 7, 0, 0, 7 * D), (0, 7, 1, C + 2 * D, 7 * D), (7, 14, 0, 7 * D, 7 * D),
                    (7, 14, 1, C + 9 * D, 7 * D), (14, 16, None, 14 * D, 4 * D)]
        ks_ready = [k_ks]
        vt_free = [k_vt]
        pb_free = [None] * 3
        stack_free = [None] * 4
        s2_at = [(-1, 3)]
        hh_free = [None] * 3
        hh_n = [0]
        m_qk = {}
        m_v = {}

        def qk_out(i, u, f0, row0, nrow, m):
            return sp.do(lambda e: e.dma_start(
                qkd[i % 2, :, f0:f0 + nrow, :].rearrange("c f n -> f c n"), HH[u][row0:row0 + nrow, :, :]),
                m, qkd_free[i % 2], sig=s_qw[u])

        def qk_in(i, p0, p1, grp, m_w):
            free = [stack_free[g] for g in range(p0 // 2, p1 // 2)]
            for kind, dst, hls in ((0, QS, (0, 1, 0)), (1, KS, (0, 0, 1))):
                for par in range(2):
                    for blk, hl in enumerate(hls):
                        f0 = kind * C + (2 * p0 + par) * D
                        src = bass.AP(qkd.tensor, qkd.offset + ((i % 2) * 2 + hl) * 2 * C * T + f0 * T,
                                      [[T, D], [2 * D * T, p1 - p0], [1, T]])
                        r0 = 64 * par + blk * D
                        m = sp.do(lambda e, dst=dst, r0=r0, src=src: e.dma_start(dst[r0:r0 + D, p0:p1, :], src),
                                  m_w, free, ks_ready[0], sig=s_qk[grp])
            m_qk[grp] = m

        qkd_free = [None, None]

        def proj_qk(i, banks=(0, 1)):
            a = A[0]
            mw = []
            for t in range(5):
                bk = banks[t % 2]
                h0, h1, kind, f0, M = QK_TILES[t]
                cols = slice(f0, f0 + M)
                tt = terms(a, [WQ[:, 0, cols], WQ[:, 1, cols]], [WQL[:, 0, cols], WQL[:, 1, cols]], WQ[:, 2, cols])
                for n, (x_, w_) in enumerate(tt):
                    mp = pe.do(lambda e, x_=x_, w_=w_, n=n, bk=bk, M=M: e.matmul(
                        PS[bk][0:M, :], r(w_), r(x_), start=(n == 0), stop=(n == 6)),
                        bank[bk], m_a[0], m_wq[0], end=(n == 6))
                u = hh_n[0] % 3
                hh_n[0] += 1
                mh = act.do(lambda e, bk=bk, M=M, u=u: e.copy(r(HH[u][0:M, 0, :]), PS[bk][0:M, :]), mp, hh_free[u])
                ml = dve.do(lambda e, bk=bk, M=M, u=u: e.tensor_tensor(
                    r(HH[u][0:M, 1, :]), PS[bk][0:M, :], HH[u][0:M, 0, :], ALU.subtract), mh, hh_free[u])
                bank[bk] = ml
                if t < 4:
                    w = qk_out(i, u, kind * C + h0 * D, 0, M, [mh, ml])
                else:
                    qk_out(i, u, 14 * D, 0, 2 * D, [mh, ml])
                    w = qk_out(i, u, C + 14 * D, 2 * D, 2 * D, None)
                hh_free[u] = w
                mw.append(w)
                yield
                if t == 1:
                    while s2_at[0] < (i - 1, 0):
                        yield
                    qk_in(i, 0, 2, 0, list(mw))
                if t == 3:
                    while s2_at[0] < (i - 1, 1):
                        yield
                    qk_in(i, 2, 4, 1, list(mw))
            while s2_at[0] < (i - 1, 3):
                yield
            qk_in(i, 4, 8, 2, mw)
            qkd_free[i % 2] = [m_qk[g] for g in range(3)]
            yield

        def proj_tok(a, ready, wh, wl, wlast, q, bk, m_w):
            tt = terms(a, wh, wl, wlast)
            for n, (x_, w_) in enumerate(tt):
                mp = pe.do(lambda e, x_=x_, w_=w_, n=n: e.matmul(
                    PS[bk][:, 0:C], r(x_[:, q * 128:(q + 1) * 128]), r(w_), start=(n == 0), stop=(n == 6)),
                    bank[bk], ready, m_w, end=(n == 6))
            return mp

        def proj_v(i):
            for q in range(QT):
                bk = 2 + q
                mp = proj_tok(A[0], m_a[0], [WV[:, 0, :], WV[:, 1, :]], [WVL[:, 0, :], WVL[:, 1, :]],
                              WV[:, 2, :], q, bk, m_wv[0])
                m_v[q] = act.do(lambda e, q=q, bk=bk: e.copy(
                    VT[:, q, 0:H * V1].rearrange("p (h d) -> p h d", d=V1)[:, :, 0:D],
                    PS[bk][:, 0:C].rearrange("p (h d) -> p h d", d=D)), mp, vt_free[0])
                bank[bk] = m_v[q]
            a_free[0] = mp
            wq_free[0] = mp

        mx_free = [None, None]
        m2_free = [None, None]
        m_mrow = {}
        s1_at = [None]

        def s1_steps(i):
            for h in range(H):
                g, hh = h // 4, h % 4
                rb, p = 64 * (h % 2), h // 2
                src = m_qk[min(g, 2)]
                for q in range(QT):
                    bk = (h * QT + q) % 2
                    mp = pe.do(lambda e, rb=rb, p=p, q=q, bk=bk: e.matmul(
                        PS[bk][:, :], r(QS[rb:rb + 54, p, q * 128:(q + 1) * 128]), r(KS[rb:rb + 54, p, :]),
                        start=True, stop=True), src, bank[bk])
                    md = dve.do(lambda e, q=q, hh=hh, g=g, bk=bk: e.reduce_max(
                        MX[g % 2][:, 8 * (hh % 2) + 4 * (hh // 2) + q:8 * (hh % 2) + 4 * (hh // 2) + q + 1], PS[bk][:, :], axis=AX.X), mp, mx_free[g % 2])
                    bank[bk] = md
                    if not (hh == 3 and q == 3):
                        yield
                bk = 0
                if hh == 3:
                    mt = pe.do(lambda e, g=g, bk=bk: e.transpose(PS[bk][0:16, 0:128], MX[g % 2][:, :], ID[:, :]),
                               md, bank[bk])
                    mx_free[g % 2] = mt
                    m1 = dve.do(lambda e, g=g, bk=bk: e.tensor_scalar(
                        r(M2[g % 2][:, 0, :]), PS[bk][0:16, 0:128], -1.0, None, ALU.mult), mt, m2_free[0])
                    m2 = dve.do(lambda e, g=g, bk=bk: e.scalar_tensor_tensor(
                        r(M2[g % 2][:, 1, :]), PS[bk][0:16, 0:128], -1.0, M2[g % 2][:, 0, :],
                        ALU.mult, ALU.subtract), m1)
                    bank[bk] = m2
                    for par in range(2):
                        for c in range(2):
                            def go(e, par=par, c=c, g=g):
                                row_ = 64 * par + 54 + c
                                return e.dma_start(
                                    QS[row_:row_ + 1, 2 * g:2 * g + 2, :].rearrange("p a (q n) -> p (a q) n", n=128),
                                    M2[g % 2][8 * par:8 * par + 8, c, :])
                            m_mrow[g] = sp.do(go, m2, stack_free[g], sig=s_m[g])
                    m2_free[0] = m_mrow[g]
                    s1_at[0] = (i, g)
                    yield

        os_free = [None]
        ot_free = [None]
        m_ot = [None] * QT
        rd_free = [None]

        def dup_o(m):
            return pool.do(lambda e: e.tensor_copy(
                OT[:, :, C:CW_].rearrange("p q (a n) -> p q a n", a=2),
                view(OT[:, :, :], 0, 256, [(1, 128, True), (CW_, QT, False), (0, 2, False), (1, 32, False)])), m)

        def at_steps(i, s1):
            state = {}

            def s2(st):
                g, kt = st // 4, st % 4
                n = st % 3
                marks = []
                for hh in range(4):
                    h = 4 * g + hh
                    rb, p, bk = 64 * (h % 2), h // 2, 2 + hh
                    mp = pe.do(lambda e, rb=rb, p=p, kt=kt, bk=bk: e.matmul(
                        PS[bk][:, :], r(KS[rb:rb + 56, p, kt * 128:(kt + 1) * 128]), r(QS[rb:rb + 56, p, :]),
                        start=True, stop=True), m_mrow[g], bank[bk])
                    me = act.do(lambda e, n=n, hh=hh, bk=bk: e.activation(
                        PB[n][:, hh, :], PS[bk][:, :], ACT.Exp, scale=SCALE),
                        mp, pb_free[n])
                    bank[bk] = me
                    marks.append(me)
                state[st] = marks
                if kt == 3:
                    stack_free[g] = mp
                    s2_at[0] = (i, g)

            def av(st):
                g, kt = st // 4, st % 4
                n = st % 3
                for hh in range(4):
                    h = 4 * g + hh
                    mp = pe.do(lambda e, h=h, hh=hh, kt=kt, n=n: e.matmul(
                        PS[6][32 * hh:32 * hh + 32, :], VT[:, kt, h * V1:h * V1 + 32], PB[n][:, hh, :],
                        start=(kt == 0), stop=(kt == 3)), state[st][hh], m_v[kt], bank[6], end=(hh == 3))
                pb_free[n] = mp
                if kt == 3:
                    mo = act.do(lambda e: e.copy(OS[:, :], PS[6][:, :]), mp, os_free[0])
                    bank[6] = mo
                    state["o", g] = mo
                return mp

            def norm_o(g):
                for q in range(QT):
                    mt = pe.do(lambda e, q=q: e.transpose(
                        PS[7][:, q * 128:(q + 1) * 128], OS[:, q * 128:(q + 1) * 128], ID[:, :]),
                        state["o", g], bank[7], end=(q == QT - 1))
                os_free[0] = mt
                v = PS[7][:, :].rearrange("p (q h d) -> p q h d", q=4, h=4)
                m1 = dve.do(lambda e: e.reciprocal(RD[:, :].rearrange("p (q h) -> p q h", q=4), v[:, :, :, D]),
                            mt, rd_free[0])
                o = OT[:, :, 72 * g:72 * g + 72].rearrange("p q (h d) -> p q h d", d=D)
                m2 = dve.do(lambda e: e.tensor_tensor(
                    o, v[:, :, :, 0:D],
                    view(RD[:, :], 0, 0, [(1, 128, True), (4, 4, False), (1, 4, False), (0, D, False)]),
                    ALU.mult), m1, ot_free[0])
                rd_free[0] = m2
                bank[7] = m2
                return m2

            for st in range(17):
                if st < 16:
                    while s1_at[0] is None or s1_at[0] < (i, st // 4):
                        next(s1)
                    s2(st)
                if st >= 1:
                    mp = av(st - 1)
                if st >= 2 and (st - 2) % 4 == 3:
                    norm_o((st - 2) // 4)
                yield
            vt_free[0] = mp
            m_ot[:] = [dup_o(norm_o(3))] * QT
            yield

        pbf = [PB[n][:, :, :].rearrange("p a n -> p (a n)") for n in range(3)]
        l2_tok = [pbf[n][:, 1152:1152 + 3 * C] for n in range(2)]
        l2_mem = [pbf[2][:, 1152:2000], VT[:, :, :].rearrange("p a n -> p (a n)")[:, 0:848]]

        l2 = {"tok": [None, None], "prod": [None] * 4, "S": [None] * 2, "E": [None] * 2, "sm": None, "o": [None] * 2, "at": (0, 0)}

        def l2_qkv(i, q):
            dst = l2_tok[q % 2]
            for j in range(3):
                bk = (3 * q + j) % 2
                if j < 2:
                    fs = slice(j * C, (j + 1) * C)
                    mp = proj_tok(A[0], m_a[0], [WQ[:, 0, fs], WQ[:, 1, fs]], [WQL[:, 0, fs], WQL[:, 1, fs]],
                                  WQ[:, 2, fs], q, bk, m_wq[0])
                else:
                    mp = proj_tok(A[0], m_a[0], [WV[:, 0, :], WV[:, 1, :]], [WVL[:, 0, :], WVL[:, 1, :]],
                                  WV[:, 2, :], q, bk, m_wv[0])
                segs = [(0, j * C, C)] if j != 1 else [(0, C + 14 * D, 2 * D), (2 * D, C, 14 * D)]
                for s0, d0, n in segs:
                    me = act.do(lambda e, bk=bk, s0=s0, d0=d0, n=n: e.copy(dst[:, d0:d0 + n], PS[bk][:, s0:s0 + n]),
                                mp, l2["tok"][q % 2], pb_free[q % 2])
                bank[bk] = me
            if q == 3:
                a_free[0] = mp
                wq_free[0] = mp
            return me

        def at2_steps(i):
            b = i % 4
            mq = {}
            mq[0] = l2_qkv(i, 0)
            mq[1] = l2_qkv(i, 1)
            def tile(q):
                tok = l2_tok[q % 2]
                wk = l2_mem[q % 2]
                wk_free = vt_free[0] if q % 2 else pb_free[2]
                S, E, O2, sm = wk[:, 0:256], wk[:, 256:512], wk[:, 512:512 + C], wk[:, 800:848]
                kv_off, vv_off = C, 2 * C
                mr = []
                for u in range(4):
                    pr = pbf[u % 3][:, 0:1152]
                    eng = pool if u == 3 else dve
                    i0 = view(tok, 0, u * 4 * D, [(1, 128, True), (D, 4, False), (0, 16, False), (1, D, False)])
                    i1 = view(tok, 0, kv_off, [(1, 128, True), (0, 4, False), (D, 16, False), (1, D, False)])
                    mpd = eng.do(lambda e, pr=pr, i0=i0, i1=i1: e.tensor_tensor(
                        pr.rearrange("p (h k d) -> p h k d", h=4, k=16), i0, i1, ALU.mult),
                        mq[q], l2["prod"][u % 3], pb_free[u % 3])
                    mr = dve.do(lambda e, pr=pr, u=u: e.tensor_reduce(
                        S[:, u * 64:(u + 1) * 64].rearrange("p (h k) -> p h k", h=4),
                        pr.rearrange("p (h k d) -> p h k d", h=4, k=16), axis=AX.X, op=ALU.add),
                        mpd, l2["S"][q % 2], wk_free)
                    l2["prod"][u % 3] = mr
                    yield
                S3 = S.rearrange("p (h k) -> p h k", h=16)
                E3 = E.rearrange("p (h k) -> p h k", h=16)
                m1 = dve.do(lambda e: e.reduce_max(sm[:, 0:16], S3, axis=AX.X), mr, l2["o"][q % 2])
                m2 = dve.do(lambda e: e.tensor_tensor(
                    S3, S3, view(sm, 0, 0, [(1, 128, True), (1, 16, False), (0, 16, False)]), ALU.subtract), m1)
                m3 = act.do(lambda e: e.activation(E, S, ACT.Exp, scale=SCALE), m2, l2["E"][q % 2])
                m4 = dve.do(lambda e: e.reduce_sum(sm[:, 16:32], E3, axis=AX.X), m3)
                m5 = dve.do(lambda e: e.reciprocal(sm[:, 32:48], sm[:, 16:32]), m4)
                l2["S"][q % 2] = m3
                yield
                for u in range(4):
                    pr = pbf[u % 3][:, 0:1152]
                    eng = pool if u == 3 else dve
                    i0 = view(E, 0, u * 64, [(1, 128, True), (16, 4, False), (0, D, False), (1, 16, False)])
                    i1 = view(tok, 0, vv_off, [(1, 128, True), (0, 4, False), (1, D, False), (D, 16, False)])
                    mpd = eng.do(lambda e, pr=pr, i0=i0, i1=i1: e.tensor_tensor(
                        pr.rearrange("p (h d k) -> p h d k", h=4, d=D), i0, i1, ALU.mult),
                        m3, l2["prod"][u % 3])
                    mr = dve.do(lambda e, pr=pr, u=u: e.tensor_reduce(
                        O2[:, u * 72:(u + 1) * 72].rearrange("p (h d) -> p h d", h=4),
                        pr.rearrange("p (h d k) -> p h d k", h=4, d=D), axis=AX.X, op=ALU.add),
                        mpd, l2["o"][q % 2])
                    l2["prod"][u % 3] = mr
                    yield
                l2["tok"][q % 2] = mr
                l2["E"][q % 2] = mr
                mo = dve.do(lambda e: e.tensor_tensor(
                    O2.rearrange("p (h d) -> p h d", d=D), O2.rearrange("p (h d) -> p h d", d=D),
                    view(sm, 0, 32, [(1, 128, True), (1, 16, False), (0, D, False)]), ALU.mult), mr, m5)
                mw = sp.do(lambda e, O2=O2, q=q: e.dma_start(
                    scr[b, :].rearrange("(h t d) -> t h d", h=H, t=T)[q * 128:(q + 1) * 128],
                    O2.rearrange("p (h d) -> p h d", d=D)), mo, sig=s_sw[q % 2])
                l2["o"][q % 2] = mw
                if q + 2 < QT:
                    mq[q + 2] = l2_qkv(i, q + 2)
                yield
            for q in range(QT):
                l2["at"] = (i, q)
                yield from tile(q)
            s2_at[0] = (i, 3)
            mr = sp.do(lambda e: e.dma_start(
                OT[:, :, 0:C], scr[b, :].rearrange("(q p c) -> p q c", p=128, c=C)),
                l2["o"], ot_free[0], sig=s_sr)
            m_ot[:] = [dup_o(mr)] * QT
            for n in range(3):
                pb_free[n] = [l2["prod"][n], l2["tok"][0], l2["tok"][1], list(l2["o"])]
            if b == 3:
                vt_free[0] = pool.do(lambda e: e.memset(VT[:, :, :], 1.0), l2["tok"][1], list(l2["o"]))
            yield

        gb_free = [None]
        m_gb = [None]

        def gates(i):
            L, b = i // 4, i % 4
            ms = []
            for g in range(2):
                bk = 6 + g
                mp = pe.do(lambda e, g=g, bk=bk: e.matmul(
                    PS[bk][:, 0:C], view(ID[:, :], 32 * (L % 2), 32 * (L % 2) + b, [(1, 4, True), (0, 128, False)]),
                    GR[32 * (L % 2):32 * (L % 2) + 4, g, :], start=True, stop=True), k_id, m_gr[L], bank[bk])
                m = act.do(lambda e, g=g, bk=bk: e.copy(GB[:, g, :], PS[bk][:, 0:C]), mp, gb_free[0])
                bank[bk] = m
                ms.append(m)
            gr_free[L % 2] = mp
            m_gb[0] = ms

        tm_free = [None, None]
        tm_n = [0]

        def residual(i, q, bk, mp, g, scalar=1.0, m_s=None):
            b = i % 4
            u = tm_n[0] % 2
            tm_n[0] += 1
            m1 = dve.do(lambda e: e.scalar_tensor_tensor(
                TM[u][:, :], PS[bk][:, 0:C], scalar, GB[:, g, :], ALU.mult, ALU.mult),
                mp, m_gb[0], m_s, tm_free[u])
            bank[bk] = m1
            m2 = pool.do(lambda e: e.tensor_tensor(
                X[:, b * QT + q, :], X[:, b * QT + q, :], TM[u][:, :], ALU.add), m1, m_x[b][q], xr[b][q])
            tm_free[u] = m2
            m_x[b][q] = m2
            return m1

        xr = [[None] * QT for _ in range(B)]

        def project(i, q):
            bk = 2 + q
            mp = proj_tok(A[1], m_a[1], [WP[:, 0, :], WP[:, 1, :]], [WPL[:, 0, :], WPL[:, 1, :]],
                          WP[:, 2, :], q, bk, m_wp[0])
            residual(i, q, bk, mp, 0)
            a_free[1] = mp
            wp_free[0] = mp

        m_cw = [None]
        cw_free = [None]

        def route(i):
            bk = 6
            for q in range(QT):
                a = A[1]
                tt = terms(a, [WG[:, 0, :], WG[:, 1, :]], [WGL[:, 0, :], WGL[:, 1, :]], WG[:, 2, :], rows=96)
                for n, (x_, w_) in enumerate(tt):
                    mp = pe.do(lambda e, x_=x_, w_=w_, n=n, q=q: e.matmul(
                        PS[bk][:, 4 * q:4 * q + 4], r(x_[:, q * 128:(q + 1) * 128]), r(w_),
                        start=(n == 0), stop=(n == 6)), bank[bk], m_a[1], m_wg[0], end=(n == 6 and q == QT - 1))
            m = dve.do(lambda e: e.tensor_copy(GL[:, :, :].rearrange("p q e -> p (q e)"), PS[bk][:, 0:16]), mp)
            bank[bk] = m
            mg = m
            m = dve.do(lambda e: e.memset(GK[:, :, :], 0.0))

            def bc(ap, n):
                return view(ap, 0, 0, [(1, 128, True), (4, QT, False), (0, n, False)])
            for j in range(4):
                for lo, hi, op in ((j + 1, 4, ALU.is_ge), (0, j, ALU.is_gt)):
                    if hi <= lo:
                        continue
                    src = view(GL[:, :, :], 0, j, [(1, 128, True), (4, QT, False), (0, hi - lo, False)])
                    m1 = dve.do(lambda e, src=src, lo=lo, hi=hi, op=op: e.tensor_tensor(
                        GC[:, :, lo:hi], src, GL[:, :, lo:hi], op), mg, m)
                    m = dve.do(lambda e, lo=lo, hi=hi: e.tensor_tensor(
                        GK[:, :, lo:hi], GK[:, :, lo:hi], GC[:, :, lo:hi], ALU.add), m1)
            m = dve.do(lambda e: e.tensor_scalar(GK[:, :, :], GK[:, :, :], 1.5, None, ALU.is_lt), m)
            m = dve.do(lambda e: e.reduce_max(GM[:, :], GL[:, :, :], axis=AX.X), m)
            m = dve.do(lambda e: e.tensor_tensor(
                GL[:, :, :], GL[:, :, :], view(GM[:, :], 0, 0, [(1, 128, True), (1, QT, False), (0, 4, False)]),
                ALU.subtract), m)
            m = act.do(lambda e: e.activation(GE[:, :, :], GL[:, :, :], ACT.Exp), m)
            m = dve.do(lambda e: e.tensor_tensor(GE[:, :, :], GE[:, :, :], GK[:, :, :], ALU.mult), m)
            m = dve.do(lambda e: e.reduce_sum(GS[:, :], GE[:, :, :], axis=AX.X), m)
            m = dve.do(lambda e: e.reciprocal(GM[:, :], GS[:, :]), m)
            m_cw[0] = dve.do(lambda e: e.tensor_tensor(
                CW[:, :, :], GE[:, :, :], view(GM[:, :], 0, 0, [(1, 128, True), (1, QT, False), (0, 4, False)]),
                ALU.mult), m, cw_free[0])

        bg = []

        def step_bg(n):
            while n > 0 and bg:
                if next(bg[0], "end") == "end":
                    bg.pop(0)
                else:
                    n -= 1


        def ffn_steps(i):
            L, b = i // 4, i % 4
            func = ACT.Gelu if L == 2 else ACT.Gelu_apprx_tanh
            a = A[1]
            for e_ in range(NE if L == 0 else 1):
                k0 = (i * NE + e_) * 3 if L == 0 else 48 + (L - 1) * 3
                last_use = L == 0 or b == 3
                hid = {}

                def fc1(j):
                    k, jj = k0 + j // 3, j % 3
                    q = k % 3
                    bk = 6 + j % 2
                    wh = [FH[q][:, c * 384 + jj * 128:c * 384 + jj * 128 + 128] for c in range(2)]
                    wl = [FL[q][:, c * 384 + jj * 128:c * 384 + jj * 128 + 128] for c in range(2)]
                    wlast = FH[q][:, F_C2 + jj * 128:F_C2 + jj * 128 + 128]
                    for n, (x_, w_) in enumerate(terms(a, wh, wl, wlast)):
                        mp = pe.do(lambda e, x_=x_, w_=w_, n=n, bk=bk: e.matmul(
                            PS[bk][:, :], r(w_), r(x_), start=(n == 0), stop=(n == 6)),
                            bank[bk], m_a[1], m_f[k], end=(n == 6))
                    f = hf_n[0] % 2
                    hf_n[0] += 1
                    u = hh_n[0] % 3
                    hh_n[0] += 1
                    mg = act.do(lambda e, f=f, bk=bk: e.activation(HF[f][:, :], PS[bk][:, :], func),
                                mp, hf_free[f])
                    bank[bk] = mg
                    mh = dve.do(lambda e, f=f, u=u: e.tensor_copy(r(HH[u][:, 0, :]), HF[f][:, :]), mg, hh_free[u])
                    ml = dve.do(lambda e, f=f, u=u: e.tensor_tensor(
                        r(HH[u][:, 1, :]), HF[f][:, :], HH[u][:, 0, :], ALU.subtract), mh)
                    hf_free[f] = ml
                    hid[j] = (u, [mh, ml])
                    return mp

                def fc2(j):
                    k, jj = k0 + j // 3, j % 3
                    q = k % 3
                    u, ready = hid[j]
                    c0 = F_FC2 + jj * C
                    wh, wl = FH[q][:, c0:c0 + C], FL[q][:, c0:c0 + C]
                    for t in range(QT):
                        tk = slice(t * 128, (t + 1) * 128)
                        if j == 0:
                            pe.do(lambda e, t=t: e.matmul(PS[2 + t][:, 0:C], r(ON[:, :]), r(B2[(k // 3) % 2][:, :]),
                                                          start=True, stop=False),
                                  bank[2 + t], m_b2[k // 3], k_on, end=False)
                        for n, (c, w_) in enumerate(((0, wh), (1, wh), (0, wl))):
                            mp = pe.do(lambda e, t=t, tk=tk, c=c, w_=w_, n=n: e.matmul(
                                PS[2 + t][:, 0:C], r(HH[u][:, c, tk]), r(w_), start=False,
                                stop=(j == NCH - 1 and n == 2)), ready,
                                end=(n == 2 and (j == NCH - 1 or t == QT - 1)))
                        if j == NCH - 1:
                            if L == 0:
                                residual(i, t, 2 + t, mp, 1, CW[:, t, e_:e_ + 1], m_cw[0])
                            else:
                                residual(i, t, 2 + t, mp, 1)
                    hh_free[u] = mp
                    if jj == 2 and last_use:
                        f_free[q] = mp
                        if j == NCH - 1:
                            b2_free[(k // 3) % 2] = mp
                        bg.append(prep_f())
                    return mp

                for j in range(NCH + 1):
                    if j < NCH:
                        m1 = fc1(j)
                        if j == NCH - 1:
                            a_last = m1
                    step_bg((1 if L == 0 else 2) if len(bg) < 2 else 4)
                    if j >= 1:
                        fc2(j - 1)
                    yield
            a_free[1] = a_last
            cw_free[0] = (s_dve, s_dve.n)
            gb_free[0] = (s_dve, s_dve.n)

        def drain(gen):
            for _ in gen:
                pass

        def weave(main, side, ratio):
            acc = 0.0
            for _ in main:
                acc += ratio
                while acc >= 1 and side is not None:
                    acc -= 1
                    if next(side, "end") == "end":
                        side = None
            return side

        def front(i):
            mn = norm(i, 0)
            yield
            xn_free[0] = yield from turn(XN, mn, 0, (i // 4, 0, i % 4), [7])

        def pre(i):
            yield from front(i)
            if i // 4 != 2:
                yield from proj_qk(i)

        def mid(i):
            L, b = i // 4, i % 4
            if i + 1 < NI and (i + 1) // 4 != 2:
                proj_v(i + 1)
            ot_free[0] = yield from turn(OT, m_ot, 1, None, [7, 6])
            for q in range(QT):
                project(i, q)
                yield
            mn = norm(i, 1)
            for _ in range(4):
                yield
            xn_free[0] = yield from turn(XN, mn, 1, (L, 2, b), [7, 6])
            mf_free[L % 2] = m_mod_last[0]
            if L == 0:
                route(i)
                yield

        load_x(0)
        drain(ada(0))
        drain(prep_q(0))
        drain(prep_v(0))
        def set_wg(m):
            m_wg[0] = m
        m_wg = [None]
        drain(split(("wg",), flat(WG), flat(WGL), 12, 8, (8, 4), lambda: None, set_wg))
        for b in range(1, B):
            load_x(b)
        drain(pre(0))
        proj_v(0)
        drain(prep_p(0))
        for _ in range(3):
            drain(prep_f())
        s1 = s1_steps(0)
        at = None
        for i in range(NI):
            L, b = i // 4, i % 4
            gates(i)
            nxt = pre(i + 1) if i + 1 < NI else iter(())
            if L == 2:
                while l2["at"] < (i, 2):
                    next(at)
                if b == 3:
                    drain(prep_q(L + 1))
                    drain(prep_v(L + 1))
                weave(at, nxt, 1.0)
            else:
                weave(at_steps(i, s1), nxt, 0.8)
            drain(nxt)
            if i + 1 < NI:
                if (i + 1) // 4 == 2:
                    at = side = at2_steps(i + 1)
                else:
                    s1 = side = s1_steps(i + 1)
            else:
                side = iter(())
            weave(mid(i), side, MID)
            if b == 1 and L < 3:
                bg.append(ada(L + 1))
            if b == 2 and L < 2:
                bg.append(prep_q(L + 1))
                bg.append(prep_v(L + 1))
            if b == 3 and L < 3:
                bg.append(prep_p(L + 1))
            weave(ffn_steps(i), side, RATIO[0] if L == 0 else RATIO[2] if (i + 1) // 4 == 2 else RATIO[1])
            step_bg(1000)
            if L == 3:
                o_v = out.rearrange("b (q p) c -> b p q c", p=128)
                mo = sp.do(lambda e, b=b: e.dma_start(o_v[b], X[:, b * QT:(b + 1) * QT, :]), m_x[b], sig=s_out)
        sp.wait(mo)
        for s in s_sw:
            sp.wait((s, s.n))
        for s in s_qw:
            sp.wait((s, s.n))

        block = ctx.enter_context(nc.Block())

        @block.sync
        def _(e):
            sp.run(e)

        @block.gpsimd
        def _(e):
            pool.run(e)

        @block.scalar
        def _(e):
            act.run(e)

        @block.vector
        def _(e):
            dve.run(e)

        @block.tensor
        def _(e):
            pe.run(e)


_NAMES = [
    ("L0_cond_", ["w_adaln", "b_adaln", "w_qkv", "b_qkv", "w_proj", "b_proj", "w1", "b1", "w2", "b2"]),
    ("L1_cond_", ["W_ada", "b_ada", "W_qkv", "b_qkv", "W_proj", "b_proj", "W_fc1", "b_fc1", "W_fc2", "b_fc2"]),
    ("L2_cond_", ["ada_w", "ada_b", "qkv_w", "qkv_b", "proj_w", "proj_b", "fc1_w", "fc1_b", "fc2_w", "fc2_b"]),
    ("L3_cond_", ["ada_w", "ada_b", "qkv_w", "qkv_b", "out_w", "out_b", "w1", "b1", "w2", "b2"]),
]


def kernel(**inputs):
    import concourse.bacc as bacc
    from concourse.bass_utils import run_bass_kernel_spmd as run

    nc = bacc.Bacc("TRN2", target_bir_lowering=False, num_devices=1, dynamic_dma_scratch_size=1024)
    arrays = {}

    def arg(name):
        a = np.ascontiguousarray(inputs[name])
        arrays["in_" + name] = a
        return nc.dram_tensor("in_" + name, a.shape, mybir.dt.from_np(a.dtype), kind="ExternalInput").ap()

    def row(ap):
        return ap.rearrange("(a n) -> a n", a=1)

    x, cond = arg("x"), arg("cond_1152")
    layers = []
    for n, (pre, names) in enumerate(_NAMES):
        a = [arg(pre + s) for s in names]
        if n == 0:
            w1 = [a[6][e] for e in range(NE)]
            b1 = [a[7][e:e + 1, :] for e in range(NE)]
            w2 = [a[8][e] for e in range(NE)]
            b2 = [a[9][e:e + 1, :] for e in range(NE)]
        else:
            w1, b1, w2, b2 = [a[6]], [row(a[7])], [a[8]], [row(a[9])]
        layers.append({"wada": a[0], "bada": row(a[1]), "wqkv": a[2], "bqkv": row(a[3]), "wo": a[4],
                       "bo": row(a[5]), "w1": w1, "b1": b1, "w2": w2, "b2": b2})
    gate_w = arg("L0_cond_w_gate")
    out = nc.dram_tensor("out_0", (B, T, C), F32, kind="ExternalOutput").ap()
    build(nc, x, cond, layers, gate_w, out)
    res = run(nc, [arrays], core_ids=[0])
    return res.results[0]["out_0"]
```

```python
import numpy as np
import concourse.bass as bass
from concourse import mybir
from contextlib import ExitStack

F32 = mybir.dt.float32
F32R = mybir.dt.float32r
ALU = mybir.AluOpType
ACT = mybir.ActivationFunctionType
AX = mybir.AxisListType

B, T, C, H, D = 4, 512, 288, 16, 18
QT = T // 128
NI = 16
NE = 4
NCH = 9
V1 = D + 1
SCALE = float(D) ** -0.5
EPS = 1e-6
R2 = 98
CW_ = 256 + 3 * 32
BIG = float(2.0 ** 100)

PRE = (1.0, 1.0)
MID = (0.2, 0.8, 0.8)
SIDE = (0.4, 1.2, 0.7)
BG = (1, 4, 1, 2)
FILL_S = (1, 3)
FILL_A = (1, 3)
LEAD = 12
W_PRE, W_MID = 2, 4
DEFER = 1
LAG = 2
RING_P = (0, 1)
RING_2 = (0, 1, 2)
RING_F = (0, 1)


def r(ap):
    return ap.bitcast(F32R)


def view(ap, part, free, dims):
    step = ap.ap[0][0]
    return bass.AP(ap.tensor, ap.offset + part * step + free,
                   [[s * step if isp else s, n] for s, n, isp in dims])


class Count:

    def __init__(self, sem, step=1):
        self.sem, self.step, self.n = sem, step, 0


class Queue:

    def __init__(self, done=None):
        self.items, self.seen, self.done = [], {}, done

    def wait(self, *marks):
        for m in marks:
            if m is None:
                continue
            if isinstance(m, list):
                self.wait(*m)
                continue
            c, v = m
            if self.seen.get(id(c), 0) < v:
                self.seen[id(c)] = v
                self.items.append(lambda e, c=c, v=v: e.wait_ge(c.sem, v))

    def do(self, fn, *marks, sig=None, end=True):
        self.wait(*marks)
        if not end:
            self.items.append(fn)
            return None
        c = sig or self.done
        c.n += c.step
        self.items.append(lambda e: fn(e).then_inc(c.sem, c.step))
        return (c, c.n)

    def run(self, e):
        for f in self.items:
            f(e)


def build(nc, x_in, cond, layers, gate_w, out):
    ctx = ExitStack()
    with ctx:
        def sb(name, shape):
            return ctx.enter_context(nc.sbuf_tensor(name, shape, F32))

        def sem(name, step=1):
            return Count(ctx.enter_context(nc.semaphore(name)), step)

        X = sb("X", [128, B * QT, C])
        A = [sb(f"A{n}", [128, 5, T]) for n in range(2)]
        WQ = sb("WQ", [128, 3, 2 * C])
        WQL = sb("WQL", [128, 2, 2 * C])
        WV = sb("WV", [128, 3, C])
        WVL = sb("WVL", [128, 2, C])
        WP = sb("WP", [128, 3, C])
        WPL = sb("WPL", [128, 2, C])
        NSC = 3 * (3 * 128) + 3 * C
        NLC = 2 * (3 * 128) + 3 * C
        FH = [sb(f"FH{n}", [128, NSC]) for n in range(3)]
        FL = [sb(f"FL{n}", [128, NLC]) for n in range(3)]
        ST = [sb(f"ST{n}", [128, NSC]) for n in range(2)]
        B2 = [sb(f"B2{n}", [2, C]) for n in range(2)]
        B2S = sb("B2S", [2, C])
        HF = [sb(f"HF{n}", [128, T]) for n in range(2)]
        HH = [sb(f"HH{n}", [128, 2, T]) for n in range(3)]
        QS = sb("QS", [128, 8, T])
        KS = sb("KS", [128, 8, T])
        VT = sb("VT", [128, QT, H * V1 + 13])
        PB = [sb(f"PB{n}", [128, 4, T]) for n in range(3)]
        OT = sb("OT", [128, QT, CW_])
        XN = sb("XN", [128, QT, CW_])
        TM = [sb(f"TM{n}", [128, C]) for n in range(2)]
        GB = sb("GB", [128, 2, C])
        GR = sb("GR", [36, 2, C])
        MF = [sb(f"MF{n}", [128, 4, 3, 4]) for n in range(2)]
        ID = sb("ID", [128, 128])
        ON = sb("ON", [2, 128])
        CT = sb("CT", [128, 3, 4])
        SL = sb("SL", [128, 3, 4])
        BN = sb("BN", [128, QT, 6])
        MV = sb("MV", [128, QT, 2])
        RS = sb("RS", [128, QT])
        NB = sb("NB", [128, QT])
        VV = sb("VV", [128, 2, QT])
        OS = sb("OS", [128, T])
        MX = [sb(f"MX{n}", [128, 16]) for n in range(2)]
        M2 = [sb("M2", [128, 2, 128])] * 2
        RD = sb("RD", [128, 16])
        WG = sb("WG", [128, 3, 4])
        WGL = sb("WGL", [128, 2, 4])
        GL = sb("GL", [128, QT, 4])
        GK = sb("GK", [128, QT, 4])
        GC = sb("GC", [128, QT, 4])
        GE = sb("GE", [128, QT, 4])
        CW = [sb(f"CW{n}", [128, QT, 4]) for n in range(2)]
        GM = sb("GM", [128, QT])
        GS = sb("GS", [128, QT])
        PS = [ctx.enter_context(nc.psum_tensor(f"PS{n}", [128, 512], F32)) for n in range(8)]
        qkd = nc.dram_tensor("qkd", [2, 2, 2 * C, T], F32, kind="Internal").ap()
        vtd = nc.dram_tensor("vtd", [T, C], F32, kind="Internal").ap()
        msk = nc.dram_tensor("msk", [2, 8, 256], F32, kind="Internal").ap()
        scr = nc.dram_tensor("scr", [B, H * T * D], F32, kind="Internal").ap()

        s_pe, s_act, s_dve, s_pool = sem("s_pe"), sem("s_act"), sem("s_dve"), sem("s_pool")
        s_x = [sem(f"s_x{b}", 16) for b in range(B)]
        s_c = sem("s_c", 16)
        s_g = sem("s_g", 16)
        s_st = [sem(f"s_st{n}", 16) for n in range(2)]
        s_b2 = sem("s_b2", 16)
        s_qk = [sem(f"s_qk{n}", 16) for n in range(3)]
        s_qw = [sem(f"s_qw{n}", 16) for n in range(3)]
        s_m = [sem(f"s_m{n}", 16) for n in range(4)]
        s_sw = [sem(f"s_sw{n}", 16) for n in range(2)]
        s_sr = sem("s_sr", 16)
        s_out = sem("s_out", 16)

        pe, act, dve, pool, sp = Queue(s_pe), Queue(s_act), Queue(s_dve), Queue(s_pool), Queue()

        bank = [None] * 8

        k_ct = pool.do(lambda e: e.memset(CT[:, :, :], 0.0))
        k_sl = pool.do(lambda e: e.memset(SL[:, :, :], 1.0))
        k_st = [pool.do(lambda e, n=n: e.memset(ST[n][:, :], 0.0)) for n in range(2)]
        m = pool.do(lambda e: e.memset(ID[:, :], 0.0))
        k_id = pool.do(lambda e: e.affine_select(out=ID[:, :], in_=ID[:, :], compare_op=ALU.not_equal,
                                                 fill=1.0, base=0, pattern=[[-1, 128]],
                                                 channel_multiplier=1), m)
        k_on = pool.do(lambda e: e.memset(ON[:, :], 1.0))
        k_a = [pool.do(lambda e, n=n: e.memset(A[n][:, 4, :], 1.0)) for n in range(2)]
        k_ks = pool.do(lambda e: e.memset(KS[:, :, :], 1.0))
        k_vt = pool.do(lambda e: e.memset(VT[:, :, :], 1.0))

        tm_free = [None, None]
        for n, (v0, v1) in enumerate(((0.0, 1.0), (-BIG, 0.0))):
            m = pool.do(lambda e, n=n, v0=v0: e.memset(TM[n][0:8, 0:256], v0))
            m = pool.do(lambda e, n=n, v1=v1: e.affine_select(
                out=TM[n][0:8, 0:256].rearrange("p (s j) -> p s j", s=8),
                in_=TM[n][0:8, 0:256].rearrange("p (s j) -> p s j", s=8), compare_op=ALU.not_equal,
                fill=v1, base=0, pattern=[[-1, 8], [0, 32]], channel_multiplier=1), m)
            k_tm = m

        m_c = None
        for c in range(3):
            n = 128 if c < 2 else 32
            m_c = sp.do(lambda e, c=c, n=n: e.dma_start(
                CT[0:n, c, :], cond[:, c * 128:c * 128 + n].rearrange("b k -> k b"),
                allow_slow_non_contiguous=True), k_ct, sig=s_c)
        m_sl = act.do(lambda e: e.activation(SL[:, 0:2, :], CT[:, 0:2, :], ACT.Silu), m_c, k_sl)
        m_sl = act.do(lambda e: e.activation(SL[0:32, 2, :], CT[0:32, 2, :], ACT.Silu))
        x_v = x_in.rearrange("b (q p) c -> b p q c", p=128)
        m_x = [None] * B

        def load_x(b):
            m = sp.do(lambda e, b=b: e.dma_start(X[:, b * QT:(b + 1) * QT, :], x_v[b]), sig=s_x[b])
            m_x[b] = [m] * QT

        st_n = [0]
        st_free = [k_st[0], k_st[1]]

        jobs = [("ada", 0, 0), ("q", 0), ("v", 0), ("ada", 0, 1), ("ada", 0, 2), ("wg",), ("p", 0)]
        jobs += [("f", k) for k in range(3)]
        k_ = 3
        for i_ in range(NI + 1):
            L_, b_ = i_ // 4, i_ % 4
            if L_ < 3 and b_ == 1:
                jobs += [("ada", L_ + 1, j) for j in range(3)]
            if L_ < 3 and b_ == 2:
                jobs += [("q", L_ + 1), ("v", L_ + 1)]
            if 1 <= i_ <= 4 or (i_ and b_ == 0):
                n_ = min(3 * NE if i_ <= 4 else 3, 4 * NE * 3 + 9 - k_)
                jobs += [("f", k) for k in range(k_, k_ + n_)]
                k_ += n_
            if L_ < 3 and b_ == 3:
                jobs += [("p", L_ + 1)]
        job_mark = {}

        def ahead():
            k = len(job_mark)
            if k >= len(jobs) or k >= st_n[0] + 2:
                return
            n = k % 2
            for dst, src in loads_of(jobs[k]):
                m = sp.do(lambda e, dst=dst, src=src, n=n: e.dma_start(dst(ST[n]), src),
                          st_free[n], sig=s_st[n])
            job_mark[k] = m

        def stage(key):
            k = st_n[0]
            assert jobs[k] == key, (jobs[k], key)
            if k not in job_mark:
                ahead()
            st_n[0] += 1
            return k % 2, job_mark[k]

        def loads_of(key):
            kind = key[0]
            if kind == "wg":
                return [
                    (lambda s: s[:, 0:8].rearrange("p (a n) -> p a n", a=2),
                     gate_w[0:256, :].rearrange("(a p) n -> p a n", a=2)),
                    (lambda s: s[0:96, 8:12], gate_w[256:288, :].unsqueeze(0).to_broadcast([3, 32, 4])),
                ]
            if kind == "f":
                L, e_, s_ = pieces[key[1]]
                w = layers[L]
                loads = w_loads(w["w1"][e_], w["b1"][e_], s_ * 384, 384, 0, 384, F_C2)
                loads.append((lambda t: t[:, F_FC2:F_C2].rearrange("p (j n) -> p j n", j=3),
                              w["w2"][e_][s_ * 384:(s_ + 1) * 384, :].rearrange("(j p) n -> p j n", j=3)))
                return loads
            w = layers[key[1]]
            if kind == "q":
                loads = []
                for src, dst, ncol in QK_COLS:
                    loads += w_loads(w["wqkv"], w["bqkv"], src, ncol, dst, 2 * C + dst, 4 * C + dst)
                return loads
            if kind == "v":
                return w_loads(w["wqkv"], w["bqkv"], 2 * C, C, 0, C, 2 * C)
            if kind == "p":
                return w_loads(w["wo"], w["bo"], 0, C, 0, C, 2 * C)
            c0 = key[2] * 2 * C
            return [
                (lambda s: s[:, 0:4 * C].rearrange("p (a n) -> p a n", a=2),
                 w["wada"][0:256, c0:c0 + 2 * C].rearrange("(a p) n -> p a n", a=2)),
                (lambda s: s[0:32, 4 * C:6 * C], w["wada"][256:288, c0:c0 + 2 * C]),
                (lambda s: s[32:33, 4 * C:6 * C], w["bada"][:, c0:c0 + 2 * C]),
            ]

        def w_loads(w, bias, c0, ncol, o0, o1, o2):
            def two(s):
                return view(s[:, :], 0, o0, [(1, 128, True), (o1 - o0, 2, False), (1, ncol, False)])
            return [
                (two, w[0:256, c0:c0 + ncol].rearrange("(a p) n -> p a n", a=2)),
                (lambda s: s[0:96, o2:o2 + ncol],
                 w[256:288, c0:c0 + ncol].unsqueeze(0).to_broadcast([3, 32, ncol])),
                (lambda s: s[96:98, o2:o2 + ncol],
                 bias[:, c0:c0 + ncol].to_broadcast([2, ncol])),
            ]

        def split(key, hi, lo, nh, nl, fix, free, done):
            n, m_ld = stage(key)
            mh = dve.do(lambda e: e.tensor_copy(r(hi), ST[n][:, 0:nh]), m_ld, free())
            ml = pool.do(lambda e: e.tensor_tensor(r(lo), ST[n][:, 0:nl], hi[:, 0:nl], ALU.subtract), mh, free())
            yield
            f0, nf = fix
            m1 = dve.do(lambda e: e.tensor_tensor(r(hi[64:R2, f0:f0 + nf]), ST[n][64:R2, f0:f0 + nf],
                                                  hi[64:R2, f0:f0 + nf], ALU.subtract), mh)
            m2 = dve.do(lambda e: e.tensor_copy(r(hi[96:97, f0:f0 + nf]), ST[n][96:97, f0:f0 + nf]), m1)
            st_free[n] = [ml, m2]
            done([ml, m2])
            yield
            ahead()
            yield

        m_wq, m_wv = [None], [None]
        m_wp = [None]
        wq_free = [None]
        wp_free = [None]

        QK_COLS = [(0, 0, C), (C + 14 * D, C, 2 * D), (C, C + 2 * D, 14 * D)]

        def flat(ap):
            return ap[:, :, :].rearrange("p a n -> p (a n)")

        def prep_q(L):
            yield from split(("q", L), flat(WQ), flat(WQL), 6 * C, 4 * C, (4 * C, 2 * C), lambda: wq_free[0],
                             lambda m: m_wq.__setitem__(0, m))

        def prep_v(L):
            yield from split(("v", L), flat(WV), flat(WVL), 3 * C, 2 * C, (2 * C, C), lambda: wq_free[0],
                             lambda m: m_wv.__setitem__(0, m))

        def prep_p(L):
            yield from split(("p", L), flat(WP), flat(WPL), 3 * C, 2 * C, (2 * C, C), lambda: wp_free[0],
                             lambda m: m_wp.__setitem__(0, m))

        pieces = [(0, e, s) for i in range(4) for e in range(NE) for s in range(3)]
        pieces += [(L, 0, s) for L in range(1, 4) for s in range(3)]
        F_FC2, F_C2 = 768, 768 + 3 * C
        m_f = {}
        f_free = [None] * 3
        b2_free = [None] * 2
        m_b2 = {}
        f_n = [0]
        b2s_free = [None]

        def prep_f():
            k = f_n[0]
            if k >= len(pieces):
                return
            f_n[0] += 1
            L, e_, s_ = pieces[k]
            q = k % 3
            if s_ == 0:
                mb = sp.do(lambda e: e.dma_start(B2S[:, :], layers[L]["b2"][e_].to_broadcast([2, C])),
                           b2s_free[0], sig=s_b2)
            yield from split(("f", k), FH[q][:, :], FL[q][:, :], NSC, NLC, (F_C2, 384), lambda: f_free[q],
                             lambda m: m_f.__setitem__(k, m))
            if s_ == 0:
                u = (k // 3) % 2
                m1 = dve.do(lambda e: e.tensor_copy(r(B2[u][:, :]), B2S[:, :]), mb, b2_free[u])
                m2 = dve.do(lambda e: e.tensor_tensor(r(B2[u][:, :]), B2S[:, :], B2[u][:, :], ALU.subtract), m1)
                m3 = dve.do(lambda e: e.tensor_copy(r(B2[u][0:1, :]), B2S[0:1, :]), m2)
                b2s_free[0] = m3
                m_b2[k // 3] = m3
                yield

        m_mf = [None] * 4
        m_gr = [None] * 4
        mf_free = [None] * 2
        gr_free = [None] * 2

        def ada(L):
            m_mf[L], m_gr[L] = marks, gm = [], []
            for j in range(3):
                n, m = stage(("ada", L, j))
                for u in range(2):
                    v = 2 * j + u
                    bk = ring()
                    if v in (2, 5):
                        for k in range(3):
                            kk = 128 if k < 2 else 33
                            mm = lambda e, k=k, kk=kk, n=n, u=u, bk=bk: e.matmul(
                                PS[bk][0:4, 0:C], SL[0:kk, k, :],
                                ST[n][0:kk, k * 2 * C + u * C:k * 2 * C + u * C + C],
                                start=(k == 0), stop=(k == 2))
                            mp = pe.do(mm, m, m_sl, bank[bk], end=(k == 2))
                        g = v // 3
                        mg = dve.do(lambda e, g=g, bk=bk: e.tensor_copy(GR[32 * (L % 2):32 * (L % 2) + 4, g, :], PS[bk][0:4, 0:C]),
                                    mp, gr_free[L % 2])
                        bank[bk] = mg
                        gm.append(mg)
                    else:
                        vi = {0: 0, 1: 1, 3: 2, 4: 3}[v]
                        for c, p0, np_ in ((0, 0, 128), (1, 0, 128), (2, 0, 32), (2, 32, 32), (2, 64, 32)):
                            for k in range(3):
                                kk = 128 if k < 2 else 33
                                base = k * 2 * C + u * C + c * 128

                                def mm(e, k=k, kk=kk, n=n, base=base, c=c, bk=bk, p0=p0, np_=np_):
                                    return e.matmul(PS[bk][p0:p0 + np_, 4 * c:4 * c + 4],
                                                    ST[n][0:kk, base:base + np_],
                                                    SL[0:kk, k, :], start=(k == 0), stop=(k == 2))
                                mp = pe.do(mm, m, m_sl, bank[bk], end=(k == 2))
                        add = 1.0 if v in (1, 4) else 0.0

                        def ev(e, vi=vi, bk=bk, add=add, p=128, c0=0, c1=2):
                            return e.tensor_scalar(MF[L % 2][0:p, vi, c0:c1, :],
                                                   PS[bk][0:p, 4 * c0:4 * c1].rearrange("p (c b) -> p c b", b=4),
                                                   add, None, ALU.add)
                        dve.do(ev, mp, mf_free[L % 2])
                        mg = dve.do(lambda e, ev=ev: ev(e, p=96, c0=2, c1=3))
                        bank[bk] = mg
                        marks.append(mg)
                    yield
                st_free[n] = mp
                ahead()
                yield

        a_free = [None, None]
        m_a = [None, None]
        bank_n = [0]
        ring_of = [RING_P]

        def ring():
            bank_n[0] += 1
            return ring_of[0][bank_n[0] % len(ring_of[0])]

        a_ready = [k_a[0], k_a[1]]
        xn_free = [None]
        hf_free = [None, None]
        hf_n = [0]
        m_mod_last = [None]

        rs_free = [None]
        xr = [[None] * QT for _ in range(B)]

        def rsqrt(m):
            i32 = mybir.dt.int32
            m = dve.do(lambda e: e.tensor_scalar(VV[:, 0, :], MV[:, :, 1], EPS, None, ALU.add), m, rs_free[0])
            m = dve.do(lambda e: e.tensor_scalar(VV[:, 1, :].bitcast(i32), VV[:, 0, :].bitcast(i32), 1, None,
                                                 ALU.logical_shift_right), m)
            m = dve.do(lambda e: e.tensor_scalar(RS[:, :].bitcast(i32), VV[:, 1, :].bitcast(i32),
                                                 -1.0, float(0x5f3759df), ALU.mult, ALU.add), m)
            for _ in range(3):
                m = dve.do(lambda e: e.tensor_tensor(VV[:, 1, :], RS[:, :], RS[:, :], ALU.mult), m)
                m = dve.do(lambda e: e.scalar_tensor_tensor(VV[:, 1, :], VV[:, 1, :], -0.5, VV[:, 0, :],
                                                            ALU.mult, ALU.mult), m)
                m = dve.do(lambda e: e.scalar_tensor_tensor(RS[:, :], VV[:, 1, :], 1.5, RS[:, :],
                                                            ALU.add, ALU.mult), m)
                yield
            return m


        def norm(i, which):
            b = i % 4
            for q in range(QT):
                m1 = dve.do(lambda e, q=q: e.bn_stats(BN[:, q, :], X[:, b * QT + q, :]), m_x[b][q])
                m2 = dve.do(lambda e, q=q: e.bn_aggr(MV[:, q, :], BN[:, q, :]), m1)
            yield
            m3 = yield from rsqrt(m2)
            m3 = dve.do(lambda e: e.scalar_tensor_tensor(NB[:, :], MV[:, :, 0], -1.0, RS[:, :], ALU.mult, ALU.mult),
                        m3)
            out_ = []
            for q in range(QT):
                act.do(lambda e, q=q: e.activation(
                    XN[:, q, 0:256], X[:, b * QT + q, 0:256], ACT.Identity,
                    bias=NB[:, q:q + 1], scale=RS[:, q:q + 1]), m3, xn_free[0])
                out_.append(act.do(lambda e, q=q: e.activation(
                    XN[:, q, 256:CW_].rearrange("p (a n) -> p a n", a=3),
                    view(X[:, :, :], 0, (b * QT + q) * C + 256, [(1, 128, True), (0, 3, False), (1, 32, False)]),
                    ACT.Identity, bias=NB[:, q:q + 1], scale=RS[:, q:q + 1])))
            rs_free[0] = out_[-1]
            xr[b] = out_
            return out_

        def turn(src, m_src, slot, mod, banks):
            a = A[slot]
            m_a[slot] = done = []
            for c in range(3):
                bk = banks[c % len(banks)] if banks else ring()
                np_ = 128 if c < 2 else 96
                for q in range(QT):
                    def tr(e, c=c, q=q, bk=bk):
                        if c < 2:
                            return e.transpose(PS[bk][:, q * 128:(q + 1) * 128],
                                               src[:, q, c * 128:(c + 1) * 128], ID[:, :])
                        return e.transpose(PS[bk][0:96, q * 128:(q + 1) * 128], src[:, q, 256:CW_], ID[:, :])
                    mp = pe.do(tr, m_src[q], k_id, bank[bk], end=(q == QT - 1))
                hi = a[0:np_, [0, 1, 4][c], :]
                if mod is None:
                    mh = act.do(lambda e, bk=bk, hi=hi, np_=np_: e.copy(r(hi), PS[bk][0:np_, :]),
                                mp, a_free[slot], a_ready[slot])
                    full, ready = (lambda p0, p1, bk=bk: PS[bk][p0:p1, :]), mh
                    eng = dve
                else:
                    L, v, b = mod
                    f = hf_n[0] % 2
                    hf_n[0] += 1
                    mfull = act.do(lambda e, bk=bk, f=f, np_=np_, c=c: e.activation(
                        HF[f][0:np_, :], PS[bk][0:np_, :], ACT.Identity,
                        scale=MF[L % 2][0:np_, v + 1, c, b:b + 1], bias=MF[L % 2][0:np_, v, c, b:b + 1]),
                        mp, m_mf[L], hf_free[f])
                    bank[bk] = mfull
                    m_mod_last[0] = mfull
                    mh = dve.do(lambda e, f=f, hi=hi, np_=np_: e.tensor_copy(r(hi), HF[f][0:np_, :]),
                                mfull, a_free[slot], a_ready[slot])
                    full, ready = (lambda p0, p1, f=f: HF[f][p0:p1, :]), mh
                    eng = dve
                if c < 2:
                    ml = eng.do(lambda e, full=full, c=c: e.tensor_tensor(
                        r(a[:, 2 + c, :]), full(0, 128), a[:, c, :], ALU.subtract), ready, a_free[slot])
                else:
                    ml = eng.do(lambda e, full=full: e.tensor_tensor(
                        r(a[32:64, 4, :]), full(32, 64), a[32:64, 4, :], ALU.subtract), ready)
                if mod is None:
                    bank[bk] = ml
                else:
                    hf_free[f] = ml
                done += [mh, ml]
                yield
            return mp

        def terms(a, wh, wl, wlast, rows=R2):
            return [(a[:, 0, :], wh[0]), (a[:, 1, :], wh[1]), (a[:, 2, :], wh[0]), (a[:, 3, :], wh[1]),
                    (a[:, 0, :], wl[0]), (a[:, 1, :], wl[1]), (a[0:rows, 4, :], wlast[0:rows])]

        QK_TILES = [(0, 7, 0, 0, 7 * D), (0, 7, 1, C + 2 * D, 7 * D), (7, 14, 0, 7 * D, 7 * D),
                    (7, 14, 1, C + 9 * D, 7 * D), (14, 16, None, 14 * D, 4 * D)]
        ks_ready = [k_ks]
        vt_free = [k_vt]
        pb_free = [None] * 3
        stack_free = [None] * 4
        s2_at = [(-1, 3)]
        hh_free = [None] * 3
        hh_n = [0]
        m_qk = {}
        m_qw = {}
        m_v = {}

        def qk_out(i, u, f0, row0, nrow, m):
            return sp.do(lambda e: e.dma_start(
                qkd[i % 2, :, f0:f0 + nrow, :].rearrange("c f n -> f c n"), HH[u][row0:row0 + nrow, :, :]),
                m, qkd_free[i % 2], sig=s_qw[u])

        def qk_in(i, p0, p1, grp, m_w):
            free = list(stack_free) if i == 12 else stack_free[p0 // 2:p1 // 2]
            for kind, dst, hls in ((0, QS, (0, 1, 0)), (1, KS, (0, 0, 1))):
                for par in range(2):
                    for blk, hl in enumerate(hls):
                        f0 = kind * C + (2 * p0 + par) * D
                        src = bass.AP(qkd.tensor, qkd.offset + ((i % 2) * 2 + hl) * 2 * C * T + f0 * T,
                                      [[T, D], [2 * D * T, p1 - p0], [1, T]])
                        r0 = 64 * par + blk * D
                        m = sp.do(lambda e, dst=dst, r0=r0, src=src: e.dma_start(dst[r0:r0 + D, p0:p1, :], src),
                                  m_w, free, ks_ready[0], sig=s_qk[grp])
            m_qk[grp] = m

        qkd_free = [None, None]

        def proj_qk(i):
            a = A[i % 2]
            mw = []
            for t in range(5):
                bk = ring()
                h0, h1, kind, f0, M = QK_TILES[t]
                cols = slice(f0, f0 + M)
                tt = terms(a, [WQ[:, 0, cols], WQ[:, 1, cols]], [WQL[:, 0, cols], WQL[:, 1, cols]], WQ[:, 2, cols])
                for n, (x_, w_) in enumerate(tt):
                    mp = pe.do(lambda e, x_=x_, w_=w_, n=n, bk=bk, M=M: e.matmul(
                        PS[bk][0:M, :], r(w_), r(x_), start=(n == 0), stop=(n == 6)),
                        bank[bk], m_a[i % 2], m_wq[0], end=(n == 6))
                u = hh_n[0] % 3
                hh_n[0] += 1
                mh = act.do(lambda e, bk=bk, M=M, u=u: e.copy(r(HH[u][0:M, 0, :]), PS[bk][0:M, :]), mp, hh_free[u])
                ml = dve.do(lambda e, bk=bk, M=M, u=u: e.tensor_tensor(
                    r(HH[u][0:M, 1, :]), PS[bk][0:M, :], HH[u][0:M, 0, :], ALU.subtract), mh, hh_free[u])
                bank[bk] = ml
                if t < 4:
                    w = qk_out(i, u, kind * C + h0 * D, 0, M, [mh, ml])
                else:
                    qk_out(i, u, 14 * D, 0, 2 * D, [mh, ml])
                    w = qk_out(i, u, C + 14 * D, 2 * D, 2 * D, None)
                hh_free[u] = w
                mw.append(w)
                yield
                if t == 1 and i // 4 != 2:
                    while s2_at[0] < (i - 1, 3 if i == 12 else 0):
                        yield
                    qk_in(i, 0, 2, 0, list(mw))
                if t == 3 and i // 4 != 2:
                    while s2_at[0] < (i - 1, 3 if i == 12 else 1):
                        yield
                    qk_in(i, 2, 4, 1, list(mw))
            m_qw[i % 2] = mw
            if i // 4 == 2:
                yield from stack_in2(i)
                return
            while s2_at[0] < (i - 1, 3):
                yield
            qk_in(i, 4, 8, 2, mw)
            qkd_free[i % 2] = [m_qk[g] for g in range(3)]
            yield

        def proj_tok(a, ready, wh, wl, wlast, q, bk, m_w):
            tt = terms(a, wh, wl, wlast)
            for n, (x_, w_) in enumerate(tt):
                mp = pe.do(lambda e, x_=x_, w_=w_, n=n: e.matmul(
                    PS[bk][:, 0:C], r(x_[:, q * 128:(q + 1) * 128]), r(w_), start=(n == 0), stop=(n == 6)),
                    bank[bk], ready, m_w, end=(n == 6))
            return mp

        def proj_v(i):
            for q in range(QT):
                bk = 2 + q
                mp = proj_tok(A[i % 2], m_a[i % 2], [WV[:, 0, :], WV[:, 1, :]], [WVL[:, 0, :], WVL[:, 1, :]],
                              WV[:, 2, :], q, bk, m_wv[0])
                m_v[q] = act.do(lambda e, q=q, bk=bk: e.copy(
                    VT[:, q, 0:H * V1].rearrange("p (h d) -> p h d", d=V1)[:, :, 0:D],
                    PS[bk][:, 0:C].rearrange("p (h d) -> p h d", d=D)), mp, vt_free[0])
                bank[bk] = m_v[q]
            a_free[i % 2] = mp
            wq_free[0] = mp

        mx_free = [None, None]
        m2_free = [None, None]
        m_mrow = {}
        s1_at = [None]

        def s1_steps(i):
            def rows(g, md):
                bk = ring()
                mt = pe.do(lambda e: e.transpose(PS[bk][0:16, 0:128], MX[g % 2][:, :], ID[:, :]), md, bank[bk])
                mx_free[g % 2] = mt
                m1 = dve.do(lambda e: e.tensor_scalar(
                    r(M2[g % 2][0:16, 0, :]), PS[bk][0:16, 0:128], -1.0, None, ALU.mult), mt, m2_free[0])
                m2 = dve.do(lambda e: e.scalar_tensor_tensor(
                    r(M2[g % 2][0:16, 1, :]), PS[bk][0:16, 0:128], -1.0, M2[g % 2][0:16, 0, :],
                    ALU.mult, ALU.subtract), m1)
                bank[bk] = m2
                for par in range(2):
                    for c in range(2):
                        def go(e, par=par, c=c):
                            row_ = 64 * par + 54 + c
                            return e.dma_start(
                                QS[row_:row_ + 1, 2 * g:2 * g + 2, :].rearrange("p a (q n) -> p (a q) n", n=128),
                                M2[g % 2][8 * par:8 * par + 8, c, :])
                        m_mrow[g] = sp.do(go, m2, stack_free[g], sig=s_m[g])
                m2_free[0] = m_mrow[g]
                s1_at[0] = (i, g)

            late = None
            for h in range(H):
                g, hh = h // 4, h % 4
                rb, p = 64 * (h % 2), h // 2
                src = m_qk[min(g, 2)]
                for q in range(QT):
                    bk = ring()
                    col = 8 * (hh % 2) + 4 * (hh // 2) + q
                    mp = pe.do(lambda e, rb=rb, p=p, q=q, bk=bk: e.matmul(
                        PS[bk][:, :], r(QS[rb:rb + 54, p, q * 128:(q + 1) * 128]), r(KS[rb:rb + 54, p, :]),
                        start=True, stop=True), src, bank[bk])
                    md = dve.do(lambda e, g=g, col=col, bk=bk: e.reduce_max(
                        MX[g % 2][:, col:col + 1], PS[bk][:, :], axis=AX.X), mp, mx_free[g % 2])
                    bank[bk] = md
                    yield
                    if late is not None and q == DEFER:
                        rows(*late)
                        late = None
                        yield
                if hh == 3:
                    late = (g, md)
            yield
            rows(*late)
            yield

        os_free = [None]
        ot_free = [None]
        m_ot = [None] * QT
        rd_free = [None]

        def dup_o(m):
            return pool.do(lambda e: e.tensor_copy(
                OT[:, :, C:CW_].rearrange("p q (a n) -> p q a n", a=2),
                view(OT[:, :, :], 0, 256, [(1, 128, True), (CW_, QT, False), (0, 2, False), (1, 32, False)])), m)

        def at_steps(i, s1):
            state = {}

            def s2(st):
                g, kt = st // 4, st % 4
                n = st % 3
                marks = []
                for hh in range(4):
                    h = 4 * g + hh
                    rb, p, bk = 64 * (h % 2), h // 2, 2 + hh
                    mp = pe.do(lambda e, rb=rb, p=p, kt=kt, bk=bk: e.matmul(
                        PS[bk][:, :], r(KS[rb:rb + 56, p, kt * 128:(kt + 1) * 128]), r(QS[rb:rb + 56, p, :]),
                        start=True, stop=True), m_mrow[g], bank[bk])
                    me = act.do(lambda e, n=n, hh=hh, bk=bk: e.activation(
                        PB[n][:, hh, :], PS[bk][:, :], ACT.Exp, scale=SCALE),
                        mp, pb_free[n])
                    bank[bk] = me
                    marks.append(me)
                    if hh in FILL_S:
                        next(s1, None)
                state[st] = marks
                if kt == 3:
                    stack_free[g] = mp
                    s2_at[0] = (i, g)

            def av(st):
                g, kt = st // 4, st % 4
                n = st % 3
                for hh in range(4):
                    h = 4 * g + hh
                    mp = pe.do(lambda e, h=h, hh=hh, kt=kt, n=n: e.matmul(
                        PS[6][32 * hh:32 * hh + 32, :], VT[:, kt, h * V1:h * V1 + 32], PB[n][:, hh, :],
                        start=(kt == 0), stop=(kt == 3)), state[st][hh], m_v[kt], bank[6], end=(hh == 3))
                    if hh in FILL_A:
                        next(s1, None)
                pb_free[n] = mp
                if kt == 3:
                    mo = act.do(lambda e: e.copy(OS[:, :], PS[6][:, :]), mp, os_free[0])
                    bank[6] = mo
                    state["o", g] = mo
                return mp

            def norm_o(g):
                for q in range(QT):
                    mt = pe.do(lambda e, q=q: e.transpose(
                        PS[7][:, q * 128:(q + 1) * 128], OS[:, q * 128:(q + 1) * 128], ID[:, :]),
                        state["o", g], bank[7], end=(q == QT - 1))
                os_free[0] = mt
                v = PS[7][:, :].rearrange("p (q h d) -> p q h d", q=4, h=4)
                m1 = dve.do(lambda e: e.reciprocal(RD[:, :].rearrange("p (q h) -> p q h", q=4), v[:, :, :, D]),
                            mt, rd_free[0])
                o = OT[:, :, 72 * g:72 * g + 72].rearrange("p q (h d) -> p q h d", d=D)
                m2 = dve.do(lambda e: e.tensor_tensor(
                    o, v[:, :, :, 0:D],
                    view(RD[:, :], 0, 0, [(1, 128, True), (4, 4, False), (1, 4, False), (0, D, False)]),
                    ALU.mult), m1, ot_free[0])
                rd_free[0] = m2
                bank[7] = m2
                return m2

            for st in range(17):
                if st < 16:
                    while s1_at[0] is None or s1_at[0] < (i, st // 4):
                        next(s1)
                    if i == 0 and st == 0:
                        for _ in range(LEAD):
                            next(s1)
                    s2(st)
                if st >= 1:
                    mp = av(st - 1)
                if st >= 2 and (st - 2) % 4 == 3:
                    norm_o((st - 2) // 4)
                yield
            vt_free[0] = mp
            m_ot[:] = [dup_o(norm_o(3))] * QT
            yield

        vtd_free = [None]
        hf_vw = [sem(f"s_vw{n}", 16) for n in range(2)]
        s_vr = sem("s_vr", 16)
        pbf = [PB[n][:, :, :].rearrange("p a n -> p (a n)") for n in range(3)]
        VF = VT[:, :, :].rearrange("p a n -> p (a n)")
        o_free = [None]

        def stack_in2(i):
            for blk in range(2):
                while s2_at[0] < (i - 1, 2 * blk + 1 if i % 4 else 3):
                    yield
                free = stack_free[2 * blk:2 * blk + 2] if i % 4 else list(stack_free)
                if i % 4 == 0:
                    for c, dst in ((0, QS), (1, KS)):
                        sp.do(lambda e, c=c, dst=dst, blk=blk: e.dma_start(
                            dst[64 * blk + 54:64 * blk + 62, :, :].rearrange("p a (z n) -> p (a z) n", n=256),
                            bass.AP(msk.tensor, msk.offset + c * 2048, [[256, 8], [0, 16], [1, 256]])),
                            m_msk, free, ks_ready[0], sig=s_qk[blk])
                for kind, dst, hls in ((0, QS, (0, 1, 0)), (1, KS, (0, 0, 1))):
                    for n, hl in enumerate(hls):
                        src = bass.AP(qkd.tensor, qkd.offset + ((i % 2) * 2 + hl) * 2 * C * T + kind * C * T + 256 * blk,
                                      [[T, D], [D * T, H], [1, 256]])
                        r0 = 64 * blk + n * D
                        m = sp.do(lambda e, dst=dst, r0=r0, src=src: e.dma_start(
                            dst[r0:r0 + D, :, :].rearrange("p a (z n) -> p (a z) n", n=256), src),
                            m_qw[i % 2], free, ks_ready[0], sig=s_qk[blk])
                m_qk[blk] = m
            qkd_free[i % 2] = [m_qk[0], m_qk[1]]

        def proj_v2(i):
            mw = []
            if i % 4 == 0:
                vt_free[0] = pool.do(lambda e: e.memset(VT[:, :, :], 1.0), vt_free[0])
            for q in range(QT):
                bk = 2 + q
                mp = proj_tok(A[i % 2], m_a[i % 2], [WV[:, 0, :], WV[:, 1, :]], [WVL[:, 0, :], WVL[:, 1, :]],
                              WV[:, 2, :], q, bk, m_wv[0])
                f = hf_n[0] % 2
                hf_n[0] += 1
                me = act.do(lambda e, f=f, bk=bk: e.copy(HF[f][:, 0:C], PS[bk][:, 0:C]), mp, hf_free[f])
                bank[bk] = me
                m = sp.do(lambda e, f=f, q=q: e.dma_start(vtd[q * 128:(q + 1) * 128, :], HF[f][:, 0:C]),
                          me, vtd_free[0], sig=hf_vw[f])
                hf_free[f] = m
                mw.append(m)
            a_free[i % 2] = mp
            wq_free[0] = mp
            for s_ in range(8):
                for blk in range(2):
                    m = sp.do(lambda e, s_=s_, blk=blk: e.dma_start(
                        bass.AP(VF.tensor, VF.offset + s_ * VF.ap[0][0] + blk * 32 * V1,
                                [[8 * VF.ap[0][0], 16], [V1, 32], [1, D]]),
                        bass.AP(vtd.tensor, vtd.offset + (blk * 256 + s_ * 32) * C,
                                [[D, 16], [C, 32], [1, D]])),
                        mw, vt_free[0], sig=s_vr)
            m_v[0] = m
            vtd_free[0] = m

        def at2_steps(i):
            b = i % 4

            def cols(t_, blk, rows, j):
                return view(t_[:, :, :], 64 * blk, j, [(1, rows, True), (32, 128, False)])

            for blk in range(2):
                for j0 in range(0, 32, 4):
                    bk = ring()
                    for c in range(4):
                        mp = pe.do(lambda e, bk=bk, c=c, blk=blk, j=j0 + c: e.matmul(
                            PS[bk][:, c * 128:(c + 1) * 128], r(cols(QS, blk, 62, j)), r(cols(KS, blk, 62, j)),
                            start=True, stop=True), m_qk[blk], bank[bk], end=(c == 3))
                    c0 = blk * 32 + j0
                    md = dve.do(lambda e, bk=bk, c0=c0: e.reduce_max(
                        OS[:, c0:c0 + 4], PS[bk][:, :].rearrange("p (c n) -> p c n", c=4), axis=AX.X),
                        mp, os_free[0])
                    bank[bk] = md
                    yield
                cs = slice(blk * 32, blk * 32 + 32)
                m1 = dve.do(lambda e, cs=cs: e.tensor_scalar(
                    r(M2[0][:, 0, cs]), OS[:, cs], -1.0, None, ALU.mult), md, m2_free[0])
                m2 = dve.do(lambda e, cs=cs: e.scalar_tensor_tensor(
                    r(M2[0][:, 1, cs]), OS[:, cs], -1.0, M2[0][:, 0, cs], ALU.mult, ALU.subtract), m1)
                for c in range(2):
                    def go(e, c=c, blk=blk, cs=cs):
                        row_ = 64 * blk + 62 + c
                        return e.dma_start(
                            QS[row_:row_ + 1, :, :].rearrange("p a (z n) -> p (a z) n", n=32), M2[0][:, c, cs])
                    m_mrow[blk] = sp.do(go, m2, stack_free, sig=s_m[blk])
            os_free[0] = m2
            m2_free[0] = [m_mrow[0], m_mrow[1]]

            def av2(rr, ready):
                blk, n = rr // 2, rr % 2
                bk = ring()
                for c in range(16):
                    mp = pe.do(lambda e, c=c: e.matmul(
                        PS[bk][:, c * V1:(c + 1) * V1], PB[n][:, c // 4, (c % 4) * 128:(c % 4) * 128 + 128],
                        VF[:, (rr * 16 + c) * V1:(rr * 16 + c + 1) * V1], start=True, stop=True),
                        ready, bank[bk], m_v[0], end=(c == 15))
                pb_free[n] = mp
                v = PS[bk][:, 0:16 * V1].rearrange("p (c d) -> p c d", d=V1)
                m1 = dve.do(lambda e: e.reciprocal(RD[:, :], v[:, :, D]), mp, rd_free[0])
                m2 = dve.do(lambda e: e.tensor_tensor(
                    pbf[2][:, rr * 288:(rr + 1) * 288].rearrange("p (c d) -> p c d", d=D), v[:, :, 0:D],
                    view(RD[:, :], 0, 0, [(1, 128, True), (1, 16, False), (0, D, False)]), ALU.mult),
                    m1, o_free[0], pb_free[2])
                rd_free[0] = m2
                bank[bk] = m2
                if rr % 2:
                    mw[blk] = sp.do(lambda e: e.dma_start(
                        scr[b, :].rearrange("(h k s e) -> k h s e", h=H, k=2, s=8)[blk],
                        pbf[2][:, blk * 576:(blk + 1) * 576]), m2, sig=s_sw[blk])
                return mp

            mw = [None, None]
            last = None
            for rr in range(4):
                blk, n = rr // 2, rr % 2
                marks = []
                for s_ in range(4):
                    bk = ring()
                    j0 = (rr % 2) * 16 + s_ * 4
                    for c in range(4):
                        mp = pe.do(lambda e, bk=bk, c=c, blk=blk, j=j0 + c: e.matmul(
                            PS[bk][:, c * 128:(c + 1) * 128], r(cols(KS, blk, 64, j)), r(cols(QS, blk, 64, j)),
                            start=True, stop=True), m_mrow[blk], bank[bk], end=(c == 3))
                    me = act.do(lambda e, n=n, s_=s_, bk=bk: e.activation(
                        PB[n][:, s_, :], PS[bk][:, :], ACT.Exp, scale=SCALE), mp, pb_free[n])
                    bank[bk] = me
                    marks.append(me)
                    yield
                if rr % 2:
                    stack_free[2 * blk] = stack_free[2 * blk + 1] = mp
                    if i == 11 and blk == 1:
                        for p0 in (0, 64):
                            m = sp.do(lambda e, p0=p0: e.dma_start(KS[p0 + 54:p0 + 56, :, :], KS[p0 + 62:p0 + 64, :, :]),
                                      stack_free, sig=s_c)
                        ks_ready[0] = m
                    s2_at[0] = (i, 2 * blk + 1)
                if last is not None:
                    av2(*last)
                    yield
                last = (rr, marks)
            vt_free[0] = av2(*last)
            yield
            mr = sp.do(lambda e: e.dma_start(
                OT[:, :, 0:C], scr[b, :].rearrange("(q p c) -> p q c", p=128, c=C)),
                mw, ot_free[0], sig=s_sr)
            o_free[0] = list(mw)
            pb_free[2] = list(mw)
            m_ot[:] = [dup_o(mr)] * QT
            if b == 3:
                vt_free[0] = pool.do(lambda e: e.memset(VT[:, :, :], 1.0), vt_free[0])
            yield

        gb_free = [None, None]
        m_gb = [None, None]

        def gates(i, g):
            L, b = i // 4, i % 4
            bk = 6 + g
            mp = pe.do(lambda e: e.matmul(
                PS[bk][:, 0:C], view(ID[:, :], 32 * (L % 2), 32 * (L % 2) + b, [(1, 4, True), (0, 128, False)]),
                GR[32 * (L % 2):32 * (L % 2) + 4, g, :], start=True, stop=True), k_id, m_gr[L], bank[bk])
            m_gb[g] = act.do(lambda e: e.copy(GB[:, g, :], PS[bk][:, 0:C]), mp, gb_free[g])
            bank[bk] = m_gb[g]
            gr_free[L % 2] = mp

        tm_n = [0]

        def residual(i, q, bk, mp, g, scalar=1.0, m_s=None):
            b = i % 4
            u = tm_n[0] % 2
            tm_n[0] += 1
            m1 = dve.do(lambda e: e.scalar_tensor_tensor(
                TM[u][:, :], PS[bk][:, 0:C], scalar, GB[:, g, :], ALU.mult, ALU.mult),
                mp, m_gb[g], m_s, tm_free[u])
            bank[bk] = m1
            gb_free[g] = m1
            m2 = pool.do(lambda e: e.tensor_tensor(
                X[:, b * QT + q, :], X[:, b * QT + q, :], TM[u][:, :], ALU.add), m1, m_x[b][q], xr[b][q])
            tm_free[u] = m2
            m_x[b][q] = m2
            return m1

        def project(i, q):
            bk = ring()
            a = (i + 1) % 2
            mp = proj_tok(A[a], m_a[a], [WP[:, 0, :], WP[:, 1, :]], [WPL[:, 0, :], WPL[:, 1, :]],
                          WP[:, 2, :], q, bk, m_wp[0])
            residual(i, q, bk, mp, 0)
            a_free[a] = mp
            wp_free[0] = mp

        m_cw = [None, None]
        cw_free = [None, None]

        def route(i):
            bk = ring()
            for q in range(QT):
                a = A[(i + 1) % 2]
                tt = terms(a, [WG[:, 0, :], WG[:, 1, :]], [WGL[:, 0, :], WGL[:, 1, :]], WG[:, 2, :], rows=96)
                for n, (x_, w_) in enumerate(tt):
                    mp = pe.do(lambda e, x_=x_, w_=w_, n=n, q=q: e.matmul(
                        PS[bk][:, 4 * q:4 * q + 4], r(x_[:, q * 128:(q + 1) * 128]), r(w_),
                        start=(n == 0), stop=(n == 6)), bank[bk], m_a[(i + 1) % 2], m_wg[0], end=(n == 6 and q == QT - 1))
            m = dve.do(lambda e: e.tensor_copy(GL[:, :, :].rearrange("p q e -> p (q e)"), PS[bk][:, 0:16]), mp)
            bank[bk] = m
            mg = m
            yield
            m = dve.do(lambda e: e.memset(GK[:, :, :], 0.0))

            def bc(ap, n):
                return view(ap, 0, 0, [(1, 128, True), (4, QT, False), (0, n, False)])
            for j in range(4):
                for lo, hi, op in ((j + 1, 4, ALU.is_ge), (0, j, ALU.is_gt)):
                    if hi <= lo:
                        continue
                    src = view(GL[:, :, :], 0, j, [(1, 128, True), (4, QT, False), (0, hi - lo, False)])
                    m1 = dve.do(lambda e, src=src, lo=lo, hi=hi, op=op: e.tensor_tensor(
                        GC[:, :, lo:hi], src, GL[:, :, lo:hi], op), mg, m)
                    m = dve.do(lambda e, lo=lo, hi=hi: e.tensor_tensor(
                        GK[:, :, lo:hi], GK[:, :, lo:hi], GC[:, :, lo:hi], ALU.add), m1)
                yield
            m = dve.do(lambda e: e.tensor_scalar(GK[:, :, :], GK[:, :, :], 1.5, None, ALU.is_lt), m)
            m = dve.do(lambda e: e.reduce_max(GM[:, :], GL[:, :, :], axis=AX.X), m)
            m = dve.do(lambda e: e.tensor_tensor(
                GL[:, :, :], GL[:, :, :], view(GM[:, :], 0, 0, [(1, 128, True), (1, QT, False), (0, 4, False)]),
                ALU.subtract), m)
            m = act.do(lambda e: e.activation(GE[:, :, :], GL[:, :, :], ACT.Exp), m)
            yield
            yield
            m = dve.do(lambda e: e.tensor_tensor(GE[:, :, :], GE[:, :, :], GK[:, :, :], ALU.mult), m)
            m = dve.do(lambda e: e.reduce_sum(GS[:, :], GE[:, :, :], axis=AX.X), m)
            m = dve.do(lambda e: e.reciprocal(GM[:, :], GS[:, :]), m)
            m_cw[i % 2] = dve.do(lambda e: e.tensor_tensor(
                CW[i % 2][:, :, :], GE[:, :, :], view(GM[:, :], 0, 0, [(1, 128, True), (1, QT, False), (0, 4, False)]),
                ALU.mult), m, cw_free[i % 2])
            yield

        bg = []

        def step_bg(n):
            while n > 0 and bg:
                if next(bg[0], "end") == "end":
                    bg.pop(0)
                else:
                    n -= 1

        def background():
            while True:
                step_bg(1)
                yield

        back = background()


        def ffn_steps(i):
            L, b = i // 4, i % 4
            func = ACT.Gelu if L == 2 else ACT.Gelu_apprx_tanh
            a_n = (i + 1) % 2
            a = A[a_n]
            last_use = L == 0 or b == 3
            k_first = i * NE * 3 if L == 0 else 48 + (L - 1) * 3
            hid = {}

            def fc1(j):
                k, jj = k_first + j // 3, j % 3
                q = k % 3
                bk = 6 + j % 2
                wh = [FH[q][:, c * 384 + jj * 128:c * 384 + jj * 128 + 128] for c in range(2)]
                wl = [FL[q][:, c * 384 + jj * 128:c * 384 + jj * 128 + 128] for c in range(2)]
                wlast = FH[q][:, F_C2 + jj * 128:F_C2 + jj * 128 + 128]
                for n, (x_, w_) in enumerate(terms(a, wh, wl, wlast)):
                    mp = pe.do(lambda e, x_=x_, w_=w_, n=n, bk=bk: e.matmul(
                        PS[bk][:, :], r(w_), r(x_), start=(n == 0), stop=(n == 6)),
                        bank[bk], m_a[a_n], m_f[k], end=(n == 6))
                f = hf_n[0] % 2
                hf_n[0] += 1
                u = hh_n[0] % 3
                hh_n[0] += 1
                mg = act.do(lambda e, f=f, bk=bk: e.activation(HF[f][:, :], PS[bk][:, :], func),
                            mp, hf_free[f])
                bank[bk] = mg
                mh = dve.do(lambda e, f=f, u=u: e.tensor_copy(r(HH[u][:, 0, :]), HF[f][:, :]), mg, hh_free[u])
                ml = dve.do(lambda e, f=f, u=u: e.tensor_tensor(
                    r(HH[u][:, 1, :]), HF[f][:, :], HH[u][:, 0, :], ALU.subtract), mh)
                hf_free[f] = ml
                hid[j] = (u, [mh, ml])
                a_free[a_n] = mp

            def fc2(n_):
                k, jj = k_first + n_ // 3, n_ % 3
                e_, j = n_ // NCH, n_ % NCH
                q = k % 3
                u, ready = hid[n_]
                c0 = F_FC2 + jj * C
                wh, wl = FH[q][:, c0:c0 + C], FL[q][:, c0:c0 + C]
                for t in range(QT):
                    tk = slice(t * 128, (t + 1) * 128)
                    if j == 0:
                        pe.do(lambda e, t=t: e.matmul(PS[2 + t][:, 0:C], r(ON[:, :]), r(B2[(k // 3) % 2][:, :]),
                                                      start=True, stop=False),
                              bank[2 + t], m_b2[k // 3], k_on, end=False)
                    for n, (c, w_) in enumerate(((0, wh), (1, wh), (0, wl))):
                        mp = pe.do(lambda e, t=t, tk=tk, c=c, w_=w_, n=n: e.matmul(
                            PS[2 + t][:, 0:C], r(HH[u][:, c, tk]), r(w_), start=False,
                            stop=(j == NCH - 1 and n == 2)), ready,
                            end=(n == 2 and (j == NCH - 1 or t == QT - 1)))
                    if j == NCH - 1:
                        if L == 0:
                            residual(i, t, 2 + t, mp, 1, CW[i % 2][:, t, e_:e_ + 1], m_cw[i % 2])
                            cw_free[i % 2] = bank[2 + t]
                        else:
                            residual(i, t, 2 + t, mp, 1)
                    if t == 1:
                        yield
                hh_free[u] = mp
                if jj == 2 and last_use:
                    f_free[q] = mp
                    if j == NCH - 1:
                        b2_free[(k // 3) % 2] = mp
                    bg.append(prep_f())
                yield

            nj = NCH * (NE if L == 0 else 1)
            for j in range(nj + LAG):
                if j < nj:
                    fc1(j)
                    yield
                step_bg(BG[0] if L == 0 and len(bg) < 2 else BG[1] if L == 0 else BG[2] if len(bg) < 2 else BG[3])
                if j >= LAG:
                    yield from fc2(j - LAG)

        def drain(gen):
            for _ in gen:
                pass

        def weave(main, sides):
            acc = [0.0] * len(sides)
            for _ in main:
                for n, (side, ratio) in enumerate(sides):
                    acc[n] += ratio
                    while acc[n] >= 1:
                        acc[n] -= 1
                        next(side, None)

        def front(i):
            mn = yield from norm(i, 0)
            for _ in range(W_PRE):
                yield
            xn_free[0] = yield from turn(XN, mn, i % 2, (i // 4, 0, i % 4), [7])

        def pre(i):
            yield from front(i)
            yield from proj_qk(i)

        def mid(i):
            L, b = i // 4, i % 4
            ot_free[0] = yield from turn(OT, m_ot, (i + 1) % 2, None, None)
            for q in range(QT):
                project(i, q)
                yield
            mn = yield from norm(i, 1)
            for _ in range(W_MID):
                yield
            xn_free[0] = yield from turn(XN, mn, (i + 1) % 2, (L, 2, b), None)
            mf_free[L % 2] = m_mod_last[0]
            if L == 0:
                yield from route(i)

        load_x(0)
        ada0 = ada(0)
        for _ in range(3):
            next(ada0)
        drain(front(0))
        drain(prep_q(0))
        drain(proj_qk(0))
        drain(prep_v(0))
        proj_v(0)
        m_wg = [None]
        prep_g = split(("wg",), flat(WG), flat(WGL), 12, 8, (8, 4), lambda: None, lambda m: m_wg.__setitem__(0, m))
        for b in range(1, B):
            load_x(b)
        for n in range(2):
            m_msk = sp.do(lambda e, n=n: e.dma_start(msk[n], TM[n][0:8, 0:256]), k_tm, sig=s_out)
        tm_free[:] = [m_msk, m_msk]
        bg += [ada0, prep_g]
        bg += [prep_p(0)]
        s1 = s1_steps(0)
        at = None
        o_v = out.rearrange("b (q p) c -> b p q c", p=128)
        for i in range(NI + 1):
            L, b = i // 4, i % 4
            if i < NI:
                nxt = pre(i + 1) if i + 1 < NI else iter(())
                ring_of[0] = RING_2 if L == 2 else RING_P
                if i:
                    gates(i, 0)
                    gates(i - 1, 1)
                weave(at if L == 2 else at_steps(i, s1), ((nxt, PRE[0] if L == 2 else PRE[1]), (back, 1.0)))
                drain(nxt)
                step_bg(1000)
                if i == 0:
                    gates(0, 0)
                side = iter(())
                if i + 1 < NI:
                    if (i + 1) // 4 == 2:
                        proj_v2(i + 1)
                        at = side = at2_steps(i + 1)
                    else:
                        proj_v(i + 1)
                        s1 = side = s1_steps(i + 1)
                m = mid(i)
            else:
                gates(i - 1, 1)
                side = m = iter(())
            ring_of[0] = RING_F if i else RING_2
            if b == 1 and L < 3:
                bg.append(ada(L + 1))
            if b == 2 and L < 3:
                bg += [prep_q(L + 1), prep_v(L + 1)]
            kind = 0 if i - 1 < 4 else 2 if (i + 1) // 4 == 2 else 1
            if i == 0:
                bg += [prep_f(), prep_f(), prep_f()]
                weave(m, ((side, 2.0), (back, 1.0)))
            if i:
                weave(ffn_steps(i - 1), ((m, MID[kind]), (side, SIDE[kind])))
            weave(m, ((side, 2.0),))
            step_bg(1000)
            if b == 3 and L < 3:
                bg.append(prep_p(L + 1))
            if i > 12:
                mo = sp.do(lambda e, b=(i - 1) % 4: e.dma_start(o_v[b], X[:, b * QT:(b + 1) * QT, :]),
                           m_x[(i - 1) % 4], sig=s_out)
        sp.wait(mo)
        for s in s_sw:
            sp.wait((s, s.n))
        for s in s_qw:
            sp.wait((s, s.n))

        block = ctx.enter_context(nc.Block())

        @block.sync
        def _(e):
            sp.run(e)

        @block.gpsimd
        def _(e):
            pool.run(e)

        @block.scalar
        def _(e):
            act.run(e)

        @block.vector
        def _(e):
            dve.run(e)

        @block.tensor
        def _(e):
            pe.run(e)


_NAMES = [
    ("L0_cond_", ["w_adaln", "b_adaln", "w_qkv", "b_qkv", "w_proj", "b_proj", "w1", "b1", "w2", "b2"]),
    ("L1_cond_", ["W_ada", "b_ada", "W_qkv", "b_qkv", "W_proj", "b_proj", "W_fc1", "b_fc1", "W_fc2", "b_fc2"]),
    ("L2_cond_", ["ada_w", "ada_b", "qkv_w", "qkv_b", "proj_w", "proj_b", "fc1_w", "fc1_b", "fc2_w", "fc2_b"]),
    ("L3_cond_", ["ada_w", "ada_b", "qkv_w", "qkv_b", "out_w", "out_b", "w1", "b1", "w2", "b2"]),
]


def kernel(**inputs):
    import concourse.bacc as bacc
    from concourse.bass_utils import run_bass_kernel_spmd as run

    nc = bacc.Bacc("TRN2", target_bir_lowering=False, num_devices=1, dynamic_dma_scratch_size=1024)
    arrays = {}

    def arg(name):
        a = np.ascontiguousarray(inputs[name])
        arrays["in_" + name] = a
        return nc.dram_tensor("in_" + name, a.shape, mybir.dt.from_np(a.dtype), kind="ExternalInput").ap()

    def row(ap):
        return ap.rearrange("(a n) -> a n", a=1)

    x, cond = arg("x"), arg("cond_1152")
    layers = []
    for n, (pre, names) in enumerate(_NAMES):
        a = [arg(pre + s) for s in names]
        if n == 0:
            w1 = [a[6][e] for e in range(NE)]
            b1 = [a[7][e:e + 1, :] for e in range(NE)]
            w2 = [a[8][e] for e in range(NE)]
            b2 = [a[9][e:e + 1, :] for e in range(NE)]
        else:
            w1, b1, w2, b2 = [a[6]], [row(a[7])], [a[8]], [row(a[9])]
        layers.append({"wada": a[0], "bada": row(a[1]), "wqkv": a[2], "bqkv": row(a[3]), "wo": a[4],
                       "bo": row(a[5]), "w1": w1, "b1": b1, "w2": w2, "b2": b2})
    gate_w = arg("L0_cond_w_gate")
    out = nc.dram_tensor("out_0", (B, T, C), F32, kind="ExternalOutput").ap()
    build(nc, x, cond, layers, gate_w, out)
    res = run(nc, [arrays], core_ids=[0])
    return res.results[0]["out_0"]
```
